# Optimizing a Trainium2 kernel written in Bass

```python
import numpy as np
import jax
import jax.numpy as jnp

def _softmax(x, axis=-1):
    return jax.nn.softmax(x, axis=axis)

def _gelu(x):
    return jax.nn.gelu(x, approximate=True)

def _silu(x):
    return jax.nn.silu(x)

def _sigmoid(x):
    return jax.nn.sigmoid(x)

def _layernorm(x, axis=-1, eps=1e-05):
    m = jnp.mean(x, axis=axis, keepdims=True)
    v = jnp.var(x, axis=axis, keepdims=True)
    return (x - m) / jnp.sqrt(v + eps)

def _scatter_add(tgt, idx, src, axis=0):
    return tgt.at[idx].add(src)

def _segment_sum(src, seg, n):
    return jax.ops.segment_sum(src, seg, n)
kernel_name = 'mk_cond_resid_d4_seqx_r4_7ab9fc'

def setup_inputs(seed: int=0):
    np.random.seed(seed)
    _w = jnp.asarray

    def _rec_inputs():
        import jax
        import jax.numpy as jnp
        _rk = jax.random.key(seed)
        x = -1.394e-06 + 0.9999 * jax.random.normal(jax.random.fold_in(_rk, 1), (4, 512, 512), jnp.float32)
        _lenS = 512 - jax.random.randint(jax.random.fold_in(_rk, 7), (4,), 0, max(1, 512 // 4) + 1, jnp.int32)
        _lenS2 = 512 - jax.random.randint(jax.random.fold_in(_rk, 8), (4,), 0, max(1, 512 // 4) + 1, jnp.int32)
        cond_2048 = -0.00499425 + 1.0058 * jax.random.normal(jax.random.fold_in(_rk, 11), (4, 512), jnp.float32)
        return (x, cond_2048)
    x, cond_2048 = _rec_inputs()

    def _L0_cond_setup():
        import jax, jax.numpy as jnp
        import numpy as np
        B, T, D = (16, 128, 512)
        key = jax.random.key(seed)
        k0, k1, k2, k3 = jax.random.split(key, 4)
        scale = 1.0 / np.sqrt(D)
        return {'initial_state': jax.random.normal(k0, (B, D), jnp.float32), 'inputs': jax.random.normal(k1, (B, T, D), jnp.float32), 'W_ih': jax.random.normal(k2, (D, 3 * D), jnp.float32) * scale, 'W_hh': jax.random.normal(k3, (D, 3 * D), jnp.float32) * scale, 'b_ih': jnp.zeros((3 * D,), jnp.float32), 'b_hh': jnp.zeros((3 * D,), jnp.float32)}
    _L0_cond_all = _L0_cond_setup()
    _L0_cond_in = {k: v for k, v in _L0_cond_all.items() if k in ('W_ih', 'W_hh', 'b_ih', 'b_hh')}
    del _L0_cond_all

    def _L1_cond_setup():
        import jax, jax.numpy as jnp
        import numpy as np
        DT = 0.01
        EPSILON = 0.08
        ALPHA = 0.7
        BETA = 0.8
        CLAMP = 20.0
        B, T, N = (64, 128, 512)

        def _derivative(q, p, drive, coupling, bias):
            i_couple = jnp.tanh(q) @ coupling.T
            dq = q - q ** 3 / 3.0 - p + drive + i_couple + bias
            dp = EPSILON * (q + ALPHA - BETA * p)
            return (dq, dp)

        def _rk4_step(q, p, drive, coupling, bias):
            dq1, dp1 = _derivative(q, p, drive, coupling, bias)
            dq2, dp2 = _derivative(q + 0.5 * DT * dq1, p + 0.5 * DT * dp1, drive, coupling, bias)
            dq3, dp3 = _derivative(q + 0.5 * DT * dq2, p + 0.5 * DT * dp2, drive, coupling, bias)
            dq4, dp4 = _derivative(q + DT * dq3, p + DT * dp3, drive, coupling, bias)
            q_next = q + DT / 6.0 * (dq1 + 2 * dq2 + 2 * dq3 + dq4)
            p_next = p + DT / 6.0 * (dp1 + 2 * dp2 + 2 * dp3 + dp4)
            q_next = jnp.clip(q_next, -CLAMP, CLAMP)
            p_next = jnp.clip(p_next, -CLAMP, CLAMP)
            return (q_next, p_next)
        key = jax.random.key(seed)
        k1, k2, k3, k4 = jax.random.split(key, 4)
        return {'q0': jax.random.normal(k1, (B, N), dtype=jnp.float32), 'p0': jax.random.normal(k2, (B, N), dtype=jnp.float32), 'input_drive_seq': jax.random.normal(k3, (B, T, N), dtype=jnp.float32), 'coupling': jax.random.normal(k4, (N, N), dtype=jnp.float32) * 0.01, 'bias': jnp.zeros((N,), dtype=jnp.float32)}
    _L1_cond_all = _L1_cond_setup()
    _L1_cond_in = {k: v for k, v in _L1_cond_all.items() if k in ('coupling', 'bias')}
    del _L1_cond_all

    def _L2_cond_setup():
        import jax, jax.numpy as jnp
        import numpy as np
        NUM_BLOCKS = 8
        NUM_LAYERS = 4
        EPS = 1e-06
        key = jax.random.key(seed)
        ks = jax.random.split(key, 6)
        B, S, H = (4, 1024, 512)
        inputs = jax.random.normal(ks[0], (B, S, H), dtype=jnp.float32)
        query_vectors = jax.random.normal(ks[1], (NUM_LAYERS, H), dtype=jnp.float32) * 0.01
        lim = float(np.sqrt(6.0 / (H + H)))
        Wk = jax.random.uniform(ks[2], (H, H), minval=-lim, maxval=lim, dtype=jnp.float32)
        Wo = jax.random.uniform(ks[3], (H, H), minval=-lim, maxval=lim, dtype=jnp.float32)
        rms_weight = jnp.ones((H,), dtype=jnp.float32)
        ln_gamma = jnp.ones((H,), dtype=jnp.float32)
        ln_beta = jnp.zeros((H,), dtype=jnp.float32)
        return {'inputs': inputs, 'layer_idx': 1, 'rms_weight': rms_weight, 'query_vectors': query_vectors, 'Wk': Wk, 'Wo': Wo, 'ln_gamma': ln_gamma, 'ln_beta': ln_beta}
    _L2_cond_all = _L2_cond_setup()
    _L2_cond_in = {k: v for k, v in _L2_cond_all.items() if k in ('rms_weight', 'Wk', 'Wo', 'ln_gamma', 'ln_beta')}
    del _L2_cond_all

    def _L3_cond_setup():
        import jax, jax.numpy as jnp
        import numpy as np
        N, C, L_IN, L_OUT = (32, 64, 512, 512)
        key = jax.random.key(seed)
        k1, k2 = jax.random.split(key)
        inp = jax.random.normal(k1, (N, C, L_IN), dtype=jnp.float32)
        grid = jax.random.uniform(k2, (N, L_OUT), dtype=jnp.float32) * 2.0 - 1.0
        return {'input': inp, 'grid': grid, 'padding_mode': 1, 'align_corners': 1}
    _L3_cond_all = _L3_cond_setup()
    _L3_cond_in = {k: v for k, v in _L3_cond_all.items() if k in ()}
    del _L3_cond_all
    return {'x': x, 'cond_2048': cond_2048, 'L0_cond_W_ih': _L0_cond_in['W_ih'], 'L0_cond_W_hh': _L0_cond_in['W_hh'], 'L0_cond_b_ih': _L0_cond_in['b_ih'], 'L0_cond_b_hh': _L0_cond_in['b_hh'], 'L1_cond_coupling': _L1_cond_in['coupling'], 'L1_cond_bias': _L1_cond_in['bias'], 'L2_cond_rms_weight': _L2_cond_in['rms_weight'], 'L2_cond_Wk': _L2_cond_in['Wk'], 'L2_cond_Wo': _L2_cond_in['Wo'], 'L2_cond_ln_gamma': _L2_cond_in['ln_gamma'], 'L2_cond_ln_beta': _L2_cond_in['ln_beta']}

def reference(x, cond_2048, L0_cond_W_ih, L0_cond_W_hh, L0_cond_b_ih, L0_cond_b_hh, L1_cond_coupling, L1_cond_bias, L2_cond_rms_weight, L2_cond_Wk, L2_cond_Wo, L2_cond_ln_gamma, L2_cond_ln_beta):
    import jax
    import jax.numpy as jnp

    def _L0_cond_ref(initial_state, inputs, W_ih, W_hh, b_ih, b_hh):
        import jax, jax.numpy as jnp
        import numpy as np
        B, T, D = (16, 128, 512)
        "ScanOverTime(GRU cell): sequential per-timestep module call with\n            dict-state passing; merge_dict_trees stacks the per-step\n            'state_predicted' tensors along axis=1 -> [B, T, D]."

        def cell(h, x):
            gi = x @ W_ih + b_ih
            gh = h @ W_hh + b_hh
            i_r, i_z, i_n = jnp.split(gi, 3, axis=-1)
            h_r, h_z, h_n = jnp.split(gh, 3, axis=-1)
            r = jax.nn.sigmoid(i_r + h_r)
            z = jax.nn.sigmoid(i_z + h_z)
            n = jnp.tanh(i_n + r * h_n)
            h_new = (1.0 - z) * n + z * h
            return (h_new, h_new)
        xs = jnp.swapaxes(inputs, 0, 1)
        _, hs = jax.lax.scan(cell, initial_state, xs)
        return jnp.swapaxes(hs, 0, 1)

    def _L1_cond_ref(q0, p0, input_drive_seq, coupling, bias):
        import jax, jax.numpy as jnp
        import numpy as np
        DT = 0.01
        EPSILON = 0.08
        ALPHA = 0.7
        BETA = 0.8
        CLAMP = 20.0
        B, T, N = (64, 128, 512)

        def _derivative(q, p, drive, coupling, bias):
            i_couple = jnp.tanh(q) @ coupling.T
            dq = q - q ** 3 / 3.0 - p + drive + i_couple + bias
            dp = EPSILON * (q + ALPHA - BETA * p)
            return (dq, dp)

        def _rk4_step(q, p, drive, coupling, bias):
            dq1, dp1 = _derivative(q, p, drive, coupling, bias)
            dq2, dp2 = _derivative(q + 0.5 * DT * dq1, p + 0.5 * DT * dp1, drive, coupling, bias)
            dq3, dp3 = _derivative(q + 0.5 * DT * dq2, p + 0.5 * DT * dp2, drive, coupling, bias)
            dq4, dp4 = _derivative(q + DT * dq3, p + DT * dp3, drive, coupling, bias)
            q_next = q + DT / 6.0 * (dq1 + 2 * dq2 + 2 * dq3 + dq4)
            p_next = p + DT / 6.0 * (dp1 + 2 * dp2 + 2 * dp3 + dp4)
            q_next = jnp.clip(q_next, -CLAMP, CLAMP)
            p_next = jnp.clip(p_next, -CLAMP, CLAMP)
            return (q_next, p_next)
        drive_tbn = jnp.swapaxes(input_drive_seq, 0, 1)

        def scan_fn(carry, drive):
            q, p = carry
            q, p = _rk4_step(q, p, drive, coupling, bias)
            return ((q, p), q)
        (_, _), q_trace_tbn = jax.lax.scan(scan_fn, (q0, p0), drive_tbn)
        return jnp.swapaxes(q_trace_tbn, 0, 1)

    def _L2_cond_ref(inputs, layer_idx, rms_weight, query_vectors, Wk, Wo, ln_gamma, ln_beta):
        import jax, jax.numpy as jnp
        import numpy as np
        NUM_BLOCKS = 8
        NUM_LAYERS = 4
        EPS = 1e-06
        B, S, H = inputs.shape
        block_size = max(1, S // NUM_BLOCKS)
        n_blocks = S // block_size
        block_repr = inputs.reshape(B, n_blocks, block_size, H).sum(axis=2)
        keys = jnp.einsum('bnh,kh->bnk', block_repr, Wk)
        rms = jnp.sqrt(jnp.mean(keys * keys, axis=-1, keepdims=True) + EPS)
        keys = keys / rms * rms_weight
        q = query_vectors[layer_idx]
        scores = jnp.einsum('bnh,h->bn', keys, q)
        attn = jax.nn.softmax(scores, axis=-1)
        attended = jnp.einsum('bn,bnh->bh', attn, block_repr)
        attended = jnp.broadcast_to(attended[:, None, :], (B, S, H))
        proj = jnp.einsum('bsh,kh->bsk', attended, Wo)
        x = inputs + proj
        mu = jnp.mean(x, axis=-1, keepdims=True)
        var = jnp.mean((x - mu) ** 2, axis=-1, keepdims=True)
        out = (x - mu) / jnp.sqrt(var + EPS) * ln_gamma + ln_beta
        return out

    def _L3_cond_ref(input, grid, padding_mode, align_corners):
        import jax, jax.numpy as jnp
        import numpy as np
        N, C, L_IN, L_OUT = (32, 64, 512, 512)
        L = input.shape[2]
        if align_corners:
            ix = (grid + 1.0) * 0.5 * (L - 1)
        else:
            ix = ((grid + 1.0) * L - 1.0) * 0.5
        x0 = jnp.floor(ix)
        w1 = ix - x0
        w0 = 1.0 - w1
        i0 = x0.astype(jnp.int32)
        i1 = i0 + 1
        i0c = jnp.clip(i0, 0, L - 1)
        i1c = jnp.clip(i1, 0, L - 1)
        v0 = jnp.take_along_axis(input, i0c[:, None, :], axis=2)
        v1 = jnp.take_along_axis(input, i1c[:, None, :], axis=2)
        if padding_mode:
            return w0[:, None, :] * v0 + w1[:, None, :] * v1
        else:
            m0 = ((i0 >= 0) & (i0 < L)).astype(input.dtype)
            m1 = ((i1 >= 0) & (i1 < L)).astype(input.dtype)
            return (w0 * m0)[:, None, :] * v0 + (w1 * m1)[:, None, :] * v1
    x = x + _L0_cond_ref(cond_2048, x, L0_cond_W_ih, L0_cond_W_hh, L0_cond_b_ih, L0_cond_b_hh)
    x = x + _L1_cond_ref(cond_2048, cond_2048, x, L1_cond_coupling, L1_cond_bias)
    x = x + _L2_cond_ref(x, 1, L2_cond_rms_weight, cond_2048, L2_cond_Wk, L2_cond_Wo, L2_cond_ln_gamma, L2_cond_ln_beta)
    x = x + _L3_cond_ref(x, cond_2048, 1, 1)
    return x

_drawn_inputs = setup_inputs


def setup_inputs(seed=0):
    import zlib

    import numpy as np

    out = dict(_drawn_inputs(seed))
    spreads = {'L0_cond_b_ih': (0.0, 0.1),
     'L0_cond_b_hh': (0.0, 0.1),
     'L1_cond_bias': (0.0, 0.1),
     'L2_cond_rms_weight': (1.0, 0.2),
     'L2_cond_ln_gamma': (1.0, 0.2),
     'L2_cond_ln_beta': (0.0, 0.1)}
    factors = {}
    for name, (base, spread) in spreads.items():
        noise = np.random.default_rng([zlib.crc32(name.encode()), seed]).standard_normal(out[name].shape)
        drawn = base * np.exp(spread * noise) if base else spread * noise
        out[name] = jnp.asarray(drawn.astype(out[name].dtype))
    for name, factor in factors.items():
        out[name] = (out[name] * factor).astype(out[name].dtype)
    return out
```

```python
import math

import concourse.bass as bass
from concourse import mybir
from contextlib import ExitStack

fp32 = mybir.dt.float32
fp16 = mybir.dt.float16
i32 = mybir.dt.int32
ALU = mybir.AluOpType
ACT = mybir.ActivationFunctionType
AX = mybir.AxisListType

B, T, D = 4, 512, 512
P = 128
K = D // P
KB = K * B
G3 = 3 * K
GC = G3 * B

DT, EPS, ALPHA, BETA, CLAMP = 0.01, 0.08, 0.7, 0.8, 20.0
STEP = [DT / 2, DT / 2, DT, DT / 6]

BLOCKS, L2_EPS = 8, 1e-6
BLOCK = T // BLOCKS


def recovery_sums():
    def vec(p=0.0, q1=0.0, q2=0.0, q3=0.0, q4=0.0, one=0.0):
        return [p, q1, q2, q3, q4, one]

    def lin(*terms):
        return [sum(c * v[i] for c, v in terms) for i in range(6)]

    p1, one = vec(p=1), vec(one=1)
    q = [vec(q1=1), vec(q2=1), vec(q3=1), vec(q4=1)]

    def slope(qs, ps):
        return lin((EPS, qs), (EPS * ALPHA, one), (-EPS * BETA, ps))

    d1 = slope(q[0], p1)
    p2 = lin((1, p1), (DT / 2, d1))
    d2 = slope(q[1], p2)
    p3 = lin((1, p1), (DT / 2, d2))
    d3 = slope(q[2], p3)
    p4 = lin((1, p1), (DT, d3))
    d4 = slope(q[3], p4)
    pn = lin((1, p1), (DT / 6, d1), (DT / 3, d2), (DT / 3, d3), (DT / 6, d4))
    return [lin((-1, p2), (2 / DT, q[0])),
            lin((-1, p3), (1 / DT, q[0])),
            lin((-1, p4), (-2 / DT, q[0]), (2 / DT, q[1]), (4 / DT, q[2]), (2 / DT, q[3])),
            pn]


UNROLL = 4


def counts(eng, first):
    known = {}

    def at(n):
        if isinstance(first, int):
            return first + n
        if n not in known:
            known[n] = eng.snap(first + n)
        return known[n]
    return at


def build(nc, x, cond, W_ih, W_hh, b_ih, b_hh, coupling, fhn_bias, rms_w, Wk, Wo, ln_g, ln_b, out):
    ctx = ExitStack()
    with ctx:
        def sb(name, shape, dt=fp32):
            return ctx.enter_context(nc.sbuf_tensor(name, shape, dt))

        def ps(name, shape, dt=fp32):
            return ctx.enter_context(nc.psum_tensor(name, shape, dt))

        def sem(name):
            return ctx.enter_context(nc.semaphore(name))

        xT_all = sb("xT", [P, T + 2, K, B])
        xT = xT_all[:, 1:T + 1, :, :]
        gi = sb("gi", [P, B, G3, T + 2])
        whh = sb("whh", [P, 2, K, 3 * D], fp16)
        cpl = sb("cpl", [P, 2, K, D], fp16)
        wih = sb("wih", [P, K, 3 * D])
        xrow = sb("xrow", [P, 2, K, D])
        ident = sb("ident", [P, P])
        NS = KB + 2 * G3 + K
        condT = sb("condT", [P, K, B])
        bias3 = sb("bias3", [P, 4, G3])
        fbias = sb("fbias", [P, K])
        amax = sb("amax", [P, 3])
        amaxa = sb("amaxa", [P, 3])
        pow2 = sb("pow2", [P, 3])
        scale = sb("scale", [P, 3])
        sprod = sb("sprod", [P, 1])
        inv = sb("inv", [P, 2])
        kap = sb("kap", [P, 5])
        negc3 = sb("negc3", [P, 1])
        h = sb("h", [P, KB])
        hpart = sb("hpart", [P, K, 2, B], fp16)
        gates = sb("gates", [P, GC])
        rz = sb("rz", [P, 2 * KB])
        gated = sb("gated", [P, KB])
        narg = sb("narg", [P, KB])
        cand = sb("cand", [P, KB])
        omz = sb("omz", [P, KB])
        zh = sb("zh", [P, KB])
        wn = sb("wn", [P, KB])
        q1raw = sb("q1raw", [P, KB])
        q1 = sb("q1", [P, KB])
        tfull = sb("tfull", [P, KB])
        tpart = sb("tpart", [P, K, 2, B], fp16)
        sq = sb("sq", [P, 4, KB])
        cub = sb("cub", [P, KB])
        qhat = sb("qhat", [P, 4, KB])
        phat = sb("phat", [P, KB])
        x1 = sb("x1", [P, KB])
        x1keep = sb("x1keep", [P, KB])
        uscaled = sb("uscaled", [P, KB])
        uhat = sb("uhat", [P, KB])
        drive0 = sb("drive0", [P, KB])
        udrive = sb("udrive", [P, 4, KB])
        psum_p = sb("psum_p", [P, 4, KB])
        sums0 = sb("sums0", [P, 4, KB])
        sums = sb("sums", [P, 4, KB])
        term = sb("term", [P, 4, KB])
        coef = sb("coef", [P, 5, 4, KB])
        konst = sb("konst", [P, 4, KB])
        scol = sb("scol", [P, KB])
        bhat = sb("bhat", [P, KB])
        clampc = sb("clampc", [P, 2])
        ones = sb("ones", [P, KB])

        pstage = ps("pstage", [P, 1024])
        pgate = ps("pgate", [P, 1024])
        pq = ps("pq", [P, 512])
        pwork = [ps(f"pwork{i}", [P, 512]) for i in range(3)]
        stage3 = pstage[:, :].rearrange("p (s c) -> p s c", c=256)
        gate3 = pgate[:, :].rearrange("p (s c) -> p s c", c=256)
        stage_base = pstage[:, 512:512 + KB]
        gate_base = pgate[:, 512:512 + GC]
        qt = pq[:, 0:KB]
        bounce = [pstage[:, 0:512], pstage[:, 512:1024], pgate[:, 0:512], pgate[:, 512:1024]]

        small = gi[0:NS, 1, 0, 0:P]
        c_row = gi[:, 2, :, :].rearrange("p n t -> p (n t)")[:, 0:K * D].rearrange("p (n k) -> p n k", n=K)
        w_row = gi[:, 3, :, :].rearrange("p n t -> p (n t)")[:, 0:K * 3 * D].rearrange("p (k n) -> p k n", k=K)

        wih_flat = wih[:, :, :].rearrange("p k n -> p (k n)")
        wk_row = wih_flat[:, 0:K * D].rearrange("p (n d) -> p n d", n=K)
        wo_row = wih_flat[:, K * D:2 * K * D].rearrange("p (n d) -> p n d", n=K)
        x3T = wih_flat[:, 0:2 * D].rearrange("p (a k t) -> p a k t", a=2, k=K)
        ytile = wih_flat[:, 2 * D:6 * D].rearrange("p (a d) -> p a d", a=4)
        rows = xrow[:, :, :, :].rearrange("p a n d -> p (a n d)")
        grid = rows[:, 0:B * D].rearrange("p (b d) -> p b d", b=B)
        rms_row, gamma_row, beta_row, query_row = [rows[:, (B + i) * D:(B + i + 1) * D] for i in range(4)]
        space = gi[:, :, :, :].rearrange("p b n t -> p (b n t)")

        def take(at, n):
            return space[:, at * D:(at + n) * D]

        spread = take(0, B * K).rearrange("p (b k l) -> p b k l", b=B, k=K)
        normed = take(16, 8).rearrange("p (a n d) -> p a n d", a=2, n=K)
        x3 = take(24, 8).rearrange("p (a n d) -> p a n d", a=2, n=K)
        projb = take(32, 4).rearrange("p (b d) -> p b d", b=B)
        wkT = take(36, 4).rearrange("p (k n) -> p k n", k=K)
        woT = take(40, 4).rearrange("p (k n) -> p k n", k=K)
        scratch = take(44, 1)
        proj4 = take(45, 1)[0:B, :]
        keyq = take(46, 1)
        x2s_a = whh[:, 0, :, :].rearrange("p k n -> p (k n)").bitcast(fp32)[:, 0:K * D].rearrange("p (n d) -> p n d", n=K)
        x2s_b = whh[:, 1, :, :].rearrange("p k n -> p (k n)").bitcast(fp32)[:, 0:K * D].rearrange("p (n d) -> p n d", n=K)
        x2s = [x2s_a, x2s_b]
        NB = B * BLOCKS
        blk = wih_flat[:, 9 * D + P:9 * D + 2 * P].rearrange("p (k b n) -> p k b n", k=K, b=B)
        weighted = wih_flat[:, 8 * D:8 * D + K * NB].rearrange("p (k b n) -> p k b n", k=K, b=B)
        att = sb("att", [P, K, B])
        feature = sb("feature", [P, K])
        sumsq = sb("sumsq", [NB, 1])
        dot = sb("dot", [NB, 1])
        root = sb("root", [P, 4])
        newton = sb("newton", [P, 3, 4])
        score = sb("score", [NB, 1])
        srow = sb("srow", [1, 5, B, BLOCKS])
        smax = sb("smax", [1, 3, B])
        onerow = wih_flat[0:1, 9 * D:9 * D + P]
        pick = wih_flat[0:B, 10 * D:11 * D].rearrange("p (b m) -> p b m", b=B)
        stats = sb("stats", [P, 6])
        moments = sb("moments", [P, 2, K, 2])
        shift = sb("shift", [P, 2, K])
        rstd = sb("rstd", [P, 2, K])

        hn_base_ready = sem("hn_base_ready")
        small_turned = sem("small_turned")
        in_small, in_wih, in_whh, in_c = sem("in_small"), sem("in_wih"), sem("in_whh"), sem("in_c")
        in_x = [sem(f"in_x{i}") for i in range(2)]
        ident_ready, ident_raw = sem("ident_ready"), sem("ident_raw")
        amax_ready, amax_all, setup = sem("amax_ready"), sem("amax_all"), sem("setup")
        consts_ready = sem("consts_ready")
        turned, turned_used = sem("turned"), sem("turned_used")
        cturned, cturned_used = sem("cturned"), sem("cturned_used")
        gi_mm, gi_done = sem("gi_mm"), sem("gi_done")
        hi_ready, whh_ready = sem("hi_ready"), sem("whh_ready")
        xT_ready, cpl_ready, tanh0_ready = sem("xT_ready"), sem("cpl_ready"), sem("tanh0_ready")
        pool_setup = sem("pool_setup")
        clear_ready = sem("clear_ready")

        h_parts, gate_mm, gibase_ready, gate_sum = sem("h_parts"), sem("gate_mm"), sem("gibase_ready"), sem("gate_sum")
        rz_ready, gated_ready, narg_ready, cand_ready = sem("rz_ready"), sem("gated_ready"), sem("narg_ready"), sem("cand_ready")
        omz_ready, zh_ready, wn_ready, h_ready, h_hi = sem("omz_ready"), sem("zh_ready"), sem("wn_ready"), sem("h_ready"), sem("h_hi")

        t_parts = [sem(f"t_parts{s}") for s in range(4)]
        stage_mm = [sem(f"stage_mm{s}") for s in range(4)]
        stage_sum = [sem(f"stage_sum{s}") for s in range(4)]
        tanh_ready = [sem(f"tanh_ready{s}") for s in range(4)]
        sq_ready = [sem(f"sq_ready{s}") for s in range(4)]
        qhat_ready = [sem(f"qhat_ready{s}") for s in range(4)]
        cub_ready = [sem(f"cub_ready{s}") for s in range(4)]
        base_ready = [sem(f"base_ready{s}") for s in range(4)]
        term_ready = [sem(f"term_ready{s}") for s in range(4)]
        sums_ready = [sem(f"sums_ready{s}") for s in range(4)]
        q1raw_ready, q1_ready = sem("q1raw_ready"), sem("q1_ready")
        x1_ready, uscaled_ready, uhat_ready, udrive_ready = sem("x1_ready"), sem("uscaled_ready"), sem("uhat_ready"), sem("udrive_ready")
        phat_ready, psum_p_ready, sums0_ready = sem("phat_ready"), sem("psum_p_ready"), sem("sums0_ready")
        drive0_ready, x2_ready, x1keep_ready = sem("drive0_ready"), sem("x2_ready"), sem("x1keep_ready")
        out_sem = [sem(f"out_sem{i}") for i in range(2 * K)]
        in_mats, in_rows = sem("in_mats"), sem("in_rows")
        feature_ready, pick_ready = sem("feature_ready"), sem("pick_ready")
        grid_ready, dist_ready, spread_ready = sem("grid_ready"), sem("dist_ready"), sem("spread_ready")
        mats_turned, mats_ready = sem("mats_turned"), sem("mats_ready")
        blk_ready, keys_mm, sumsq_ready, dot_ready = sem("blk_ready"), sem("keys_mm"), sem("sumsq_ready"), sem("dot_ready")
        score_ready, srow_mm, sexp_in, sexp_ready = sem("score_ready"), sem("srow_mm"), sem("sexp_in"), sem("sexp_ready")
        attn_ready, attn_mm, att_ready = sem("attn_ready"), sem("attn_mm"), sem("att_ready")
        proj_mm, proj4_ready, projb_mm, projb_ready = sem("proj_mm"), sem("proj4_ready"), sem("projb_mm"), sem("projb_ready")
        var_ready, root_ready = sem("var_ready"), sem("root_ready")
        l2 = sem("l2")
        x2_turned, x2s_ready, y_ready, moments_ready = sem("x2_turned"), sem("x2s_ready"), sem("y_ready"), sem("moments_ready")
        lnvar_ready, lnroot_ready, rstd_ready = sem("lnvar_ready"), sem("lnroot_ready"), sem("rstd_ready")
        normed_ready, scaled_ready, shifted_ready, x3_ready = sem("normed_ready"), sem("scaled_ready"), sem("shifted_ready"), sem("x3_ready")
        x3_turned, x3T_ready, sample_mm, final_ready = sem("x3_turned"), sem("x3T_ready"), sem("sample_mm"), sem("final_ready")

        block = ctx.enter_context(nc.Block())

        @block.sync
        def _(sp):
            def load_x(b):
                sp.dma_start(xrow[:, b % 2, :, :], x[b].rearrange("(n p) d -> p n d", p=P)).then_inc(in_x[b % 2], 16)

            load_x(0)
            sp.dma_start(w_row, W_hh.rearrange("(k p) n -> p k n", p=P)).then_inc(in_whh, 16)
            sp.dma_start(c_row, coupling.rearrange("(n p) k -> p n k", p=P)).then_inc(in_c, 16)
            sp.dma_start(wih[:, :, :], W_ih.rearrange("(k p) n -> p k n", p=P)).then_inc(in_wih, 16)
            load_x(1)
            for b in range(2, B):
                sp.wait_ge(turned, K * (b - 1))
                load_x(b)
            sp.wait_ge(turned, B * K)
            sp.dma_start(grid.rearrange("p b d -> p (b d)"),
                         cond.rearrange("b d -> (b d)").unsqueeze(0).broadcast_to([P, B * D])).then_inc(in_rows, 16)
            for dst, src in ((rms_row, rms_w), (gamma_row, ln_g), (beta_row, ln_b), (query_row, cond[1])):
                sp.dma_start(dst, src.unsqueeze(0).broadcast_to([P, D])).then_inc(in_rows, 16)
            sp.wait_ge(gi_mm, B * G3)
            sp.dma_start(wk_row, Wk.rearrange("(n p) d -> p n d", p=P)).then_inc(in_mats, 16)
            sp.dma_start(wo_row, Wo.rearrange("(n p) d -> p n d", p=P)).then_inc(in_mats, 16)
            for e in range(B * K):
                sp.wait_ge(final_ready, e + 1)
                sp.dma_start(out[e // K, (e % K) * P:(e % K + 1) * P, :], normed[:, e // K % 2, e % K, :]).then_inc(out_sem[e % (2 * K)], 16)
            for place in range(2 * K):
                sp.wait_ge(out_sem[place], 16 * (B // 2))

        @block.gpsimd
        def _(pool):
            pool.memset(ident[:, :], 0.0).then_inc(ident_raw, 1)
            pool.wait_ge(ident_raw, 1)
            pool.affine_select(out=ident[:, :], in_=ident[:, :], compare_op=ALU.not_equal, fill=1.0, base=0,
                               pattern=[[-1, P]], channel_multiplier=1).then_inc(ident_ready, 1)
            sums_of = recovery_sums()
            for src in range(5):
                for r in range(4):
                    pool.memset(coef[:, src, r, :], sums_of[r][src])
            pool.iota(feature[:, :], pattern=[[-P, K]], base=0, channel_multiplier=-1,
                      allow_small_or_imprecise_dtypes=True).then_inc(feature_ready, 1)
            pool.memset(ones[:, :], 1.0)
            pool.memset(xT_all[:, T + 1, :, :], 0.0)
            pool.memset(x1keep[:, :], 0.0)
            pool.wait_ge(amax_ready, 3)
            pool.partition_all_reduce(amaxa[:, :], amax[:, :], P, bass.bass_isa.ReduceOp.max).then_inc(amax_all, 1)
            pool.wait_ge(phat_ready, 1)

            def keep_state(v, i=None):
                pool.wait_ge(rz_ready, v)
                pool.tensor_tensor(omz[:, :], ones[:, :], rz[:, KB:2 * KB], ALU.subtract).then_inc(omz_ready, 1)
                if not isinstance(v, int) or v > 1:
                    pool.wait_ge(h_ready, v - 1)
                pool.tensor_tensor(zh[:, :], rz[:, KB:2 * KB], h[:, :], ALU.mult).then_inc(zh_ready, 1)

            def next_drive(v, t_next):
                pool.wait_ge(h_ready, v)
                pool.tensor_tensor(x1[:, :], xT_all[:, t_next + 1, :, :].rearrange("p k b -> p (k b)"), h[:, :],
                                   ALU.add).then_inc(x1_ready, 1)
                pool.wait_ge(x1_ready, v)
                pool.tensor_tensor(uscaled[:, :], x1[:, :], scol[:, :], ALU.mult).then_inc(uscaled_ready, 1)
                pool.wait_ge(uscaled_ready, v)
                pool.tensor_tensor(uhat[:, :], uscaled[:, :], bhat[:, :], ALU.add).then_inc(uhat_ready, 1)
                pool.wait_ge(uhat_ready, v)
                pool.tensor_tensor(udrive[:, 0:3, :], konst[:, 0:3, :],
                                   uhat[:, :].unsqueeze(1).broadcast_to([P, 3, KB]), ALU.add).then_inc(udrive_ready, 1)

            def start_sums(v):
                pool.wait_ge(phat_ready, v)
                pool.tensor_tensor(drive0[:, :], uhat[:, :], phat[:, :], ALU.subtract).then_inc(drive0_ready, 1)
                pool.tensor_tensor(psum_p[:, :, :], coef[:, 0, :, :],
                                   phat[:, :].unsqueeze(1).broadcast_to([P, 4, KB]), ALU.mult).then_inc(psum_p_ready, 1)
                pool.wait_ge(psum_p_ready, v)
                pool.tensor_tensor(sums0[:, :, :], psum_p[:, :, :], udrive[:, :, :], ALU.add).then_inc(sums0_ready, 1)

            pool.wait_ge(whh_ready, 1)
            pool.wait_ge(cpl_ready, 1)
            pool.memset(gi[:, :, :, T:T + 2], 0.0).then_inc(clear_ready, 1)
            keep_state(1)
            next_drive(1, 0)
            keep_state(2)
            start_sums(1)

            def step(at, u):
                now, tail, gru = at(u + 1), at(u + 2), at(u + 3)
                pool.wait_ge(q1_ready, now)
                pool.tensor_tensor(qhat[:, 0, :], q1[:, :], scol[:, :], ALU.mult).then_inc(qhat_ready[0], 1)
                pool.wait_ge(qhat_ready[0], now)
                pool.tensor_tensor(term[:, :, :], coef[:, 1, :, :],
                                   qhat[:, 0, :].unsqueeze(1).broadcast_to([P, 4, KB]), ALU.mult).then_inc(term_ready[0], 1)
                pool.wait_ge(sums0_ready, now)
                pool.wait_ge(term_ready[0], now)
                pool.tensor_tensor(sums[:, :, :], sums0[:, :, :], term[:, :, :], ALU.add).then_inc(sums_ready[0], 1)
                for s, lo in ((1, 1), (2, 2), (3, 2)):
                    pool.wait_ge(qhat_ready[s], now)
                    pool.wait_ge(sums_ready[s - 1], now)
                    pool.tensor_tensor(term[:, lo:4, :], coef[:, 1 + s, lo:4, :],
                                       qhat[:, s, :].unsqueeze(1).broadcast_to([P, 4 - lo, KB]),
                                       ALU.mult).then_inc(term_ready[s], 1)
                    pool.wait_ge(term_ready[s], now)
                    pool.tensor_tensor(sums[:, lo:4, :], sums[:, lo:4, :], term[:, lo:4, :],
                                       ALU.add).then_inc(sums_ready[s], 1)
                    if s == 1:
                        pool.wait_ge(x2_ready, now)
                        pool.tensor_tensor(x1keep[:, :], x1[:, :], ones[:, :], ALU.mult).then_inc(x1keep_ready, 1)
                        pool.wait_ge(x1keep_ready, now)
                        next_drive(tail, now)
                start_sums(tail)
                keep_state(gru)

            with pool.Fori(0, T - UNROLL + 1, UNROLL) as t:
                at = counts(pool, t)
                for u in range(UNROLL):
                    step(at, u)

            pool.wait_ge(gi_mm, B * G3)
            pool.memset(onerow[:, :], 1.0)
            pool.memset(pick[:, :, :], 0.0).then_inc(pick_ready, 1)
            pool.wait_ge(pick_ready, 1)
            pool.affine_select(out=pick[:, :, :], in_=pick[:, :, :], compare_op=ALU.not_equal, fill=1.0, base=0,
                               pattern=[[-1, B], [0, P]], channel_multiplier=1).then_inc(pick_ready, 1)
            for b in range(B):
                for n in range(K):
                    e = b * K + n
                    pool.wait_ge(normed_ready, e + 1)
                    pool.tensor_tensor(x3[:, b % 2, n, :], normed[:, b % 2, n, :], gamma_row, ALU.mult).then_inc(scaled_ready, 1)
                    pool.wait_ge(scaled_ready, e + 1)
                    pool.tensor_tensor(x3[:, b % 2, n, :], x3[:, b % 2, n, :], beta_row, ALU.add).then_inc(shifted_ready, 1)
        @block.scalar
        def _(act):
            for src, at, n in ((cond.rearrange("b (k p) -> (b k) p", p=P), 0, KB),
                               (b_ih.rearrange("(n p) -> n p", p=P), KB, G3),
                               (b_hh.rearrange("(n p) -> n p", p=P), KB + G3, G3),
                               (fhn_bias.rearrange("(n p) -> n p", p=P), KB + 2 * G3, K)):
                act.dma_start(small[at:at + n, :], src).then_inc(in_small, 16)
            act.wait_ge(consts_ready, 1)
            for b in range(B):
                if b == 2:
                    act.wait_ge(cpl_ready, 1)
                if b == 3:
                    act.wait_ge(whh_ready, 1)
                for n in range(G3):
                    e = b * G3 + n
                    act.wait_ge(gi_mm, e + 1)
                    act.activation(gi[:, b, n, 0:T], pwork[e % 3][:, :], ACT.Identity,
                                   bias=bias3[:, 2, n:n + 1]).then_inc(gi_done, 1)
            k_gate, k_prod, k_half, k_full, k_sixth = [act.alloc_register(f"act_scale{i}") for i in range(5)]
            for n, r in enumerate((k_gate, k_prod, k_half, k_full, k_sixth)):
                act.reg_load(r, kap[0:1, n:n + 1].bitcast(i32))
            k_stage = [k_half, k_half, k_full, k_sixth]

            def gate_input(v, g, read):
                if read is not None:
                    act.wait_ge(gate_sum, read)
                act.activation(gate_base[:, 0:2 * KB].rearrange("p (n b) -> p n b", b=B),
                               gi[:, :, 0:2 * K, g].rearrange("p b n -> p n b"), ACT.Copy,
                               scale=k_prod).then_inc(gibase_ready, 1)

            def sigmoids(v):
                act.wait_ge(gate_sum, v)
                act.activation(rz[:, :], gates[:, 0:2 * KB], ACT.Sigmoid, scale=k_gate).then_inc(rz_ready, 1)

            def candidate(v):
                act.wait_ge(narg_ready, v)
                act.activation(cand[:, :], narg[:, :], ACT.Tanh).then_inc(cand_ready, 1)

            act.wait_ge(clear_ready, 1)
            act.wait_ge(hn_base_ready, 1)
            gate_input(1, 0, None)
            sigmoids(1)
            candidate(1)
            gate_input(2, 1, 1)
            sigmoids(2)
            candidate(2)
            act.activation(tpart[:, :, 0, :], condT[:, :, :], ACT.Tanh)
            act.activation(tfull[:, :], condT[:, :, :].rearrange("p k b -> p (k b)"), ACT.Tanh).then_inc(tanh0_ready, 1)

            def step(at, u):
                now, tail, gru = at(u + 1), at(u + 2), at(u + 3)
                gate_input(gru, tail, tail)
                for s in range(4):
                    act.wait_ge(stage_sum[s], now)
                    act.activation(tpart[:, :, 0, :], qt.rearrange("p (k b) -> p k b", b=B), ACT.Tanh, scale=k_stage[s])
                    act.activation(tfull[:, :], qt, ACT.Tanh, scale=k_stage[s]).then_inc(tanh_ready[s], 1)
                    if s < 3:
                        act.activation(sq[:, s + 1, :], qt, ACT.Square, scale=k_stage[s]).then_inc(sq_ready[s + 1], 1)
                        act.activation(qhat[:, s + 1, :], qt, ACT.Copy, scale=STEP[s]).then_inc(qhat_ready[s + 1], 1)
                    else:
                        act.activation(q1raw[:, :], qt, ACT.Copy, scale=k_stage[s]).then_inc(q1raw_ready, 1)
                    if s == 2:
                        sigmoids(gru)
                candidate(gru)

            with act.Fori(0, T - UNROLL + 1, UNROLL) as t:
                at = counts(act, t)
                for u in range(UNROLL):
                    step(at, u)

            for k in range(2 * K):
                act.wait_ge(mats_turned, k + 1)
                act.activation(wkT[:, k, :] if k < K else woT[:, k - K, :], bounce[k % 4], ACT.Copy).then_inc(mats_ready, 1)
            for b in range(B):
                for k in range(K):
                    act.activation(spread[:, b, k, :], grid[:, b, :], ACT.Abs, bias=feature[:, k:k + 1]).then_inc(dist_ready, 1)
            act.wait_ge(keys_mm, 1)
            act.activation(scratch[0:NB, :], pwork[0][0:NB, :], ACT.Square, accum_out=sumsq[:, :]).then_inc(sumsq_ready, 1)
            act.wait_ge(var_ready, 1)
            act.activation(root[0:NB, 0:1], newton[0:NB, 0, 0:1], ACT.Sqrt).then_inc(root_ready, 1)
            act.wait_ge(sexp_in, 1)
            act.activation(srow[:, 2, :, :], srow[:, 1, :, :], ACT.Exp).then_inc(sexp_ready, 1)
            act.wait_ge(proj_mm, 1)
            act.activation(proj4, pwork[2][0:B, :], ACT.Copy).then_inc(proj4_ready, 1)
            for b in range(B):
                act.wait_ge(projb_mm, b + 1)
                act.activation(projb[:, b, :], bounce[b], ACT.Copy).then_inc(projb_ready, 1)

            def rows_out(b):
                for n in range(K):
                    e = b * K + n
                    act.wait_ge(x2_turned, e + 1)
                    if b >= 2:
                        act.wait_ge(x3_ready, e - 2 * K + 1)
                    act.activation(x2s[b % 2][:, n, :], bounce[e % 2], ACT.Copy).then_inc(x2s_ready, 1)

            rows_out(0)

            def deviation(b):
                act.wait_ge(lnvar_ready, b + 1)
                act.activation(root[:, :], newton[:, 0, :], ACT.Sqrt).then_inc(lnroot_ready, 1)

            deviation(0)
            for b in range(B):
                act.wait_ge(rstd_ready, b + 1)
                for n in range(K):
                    e = b * K + n
                    if b >= 2:
                        act.wait_ge(out_sem[e % (2 * K)], 16)
                    act.activation(normed[:, b % 2, n, :], ytile[:, n, :], ACT.Identity, bias=shift[:, b % 2, n:n + 1],
                                   scale=rstd[:, b % 2, n:n + 1]).then_inc(normed_ready, 1)
                if b + 1 < B:
                    rows_out(b + 1)
                    deviation(b + 1)
                for n in range(K):
                    e = b * K + n
                    act.wait_ge(x3_turned, e + 1)
                    if e >= 2:
                        act.wait_ge(sample_mm, e - 1)
                    act.activation(x3T[:, e % 2, :, :].rearrange("p k t -> p (k t)"), bounce[2 + e % 2], ACT.Copy).then_inc(x3T_ready, 1)

        @block.vector
        def _(dve):
            done = [0]

            def link(ins):
                done[0] += 1
                ins.then_inc(setup, 1)
                dve.wait_ge(setup, done[0])

            def turn_x(b):
                for n in range(K):
                    e = b * K + n
                    dve.wait_ge(turned, e + 1)
                    dve.tensor_copy(xT[:, n * P:(n + 1) * P, :, b].rearrange("p t k -> p k t"),
                                    bounce[e % 4].rearrange("p (k t) -> p k t", k=K)).then_inc(xT_ready, 1)

            dve.wait_ge(small_turned, 1)
            link(dve.tensor_copy(condT[:, :, :].rearrange("p k b -> p b k"),
                                 pwork[0][:, 0:KB].rearrange("p (b k) -> p b k", k=K)))
            link(dve.tensor_copy(bias3[:, 0:2, :].rearrange("p a n -> p (a n)"), pwork[0][:, KB:KB + 2 * G3]))
            link(dve.tensor_copy(fbias[:, :], pwork[0][:, KB + 2 * G3:NS]))
            link(dve.tensor_copy(bias3[:, 2, :], bias3[:, 0, :]))
            dve.tensor_tensor(bias3[:, 2, 0:2 * K], bias3[:, 0, 0:2 * K], bias3[:, 1, 0:2 * K],
                              ALU.add).then_inc(consts_ready, 1)
            dve.tensor_reduce(amax[:, 2:3], condT[:, :, :].rearrange("p k b -> p (k b)"), AX.X, ALU.max,
                              apply_absolute_value=True).then_inc(amax_ready, 1)
            turn_x(0)
            dve.wait_ge(in_whh, 16)
            dve.tensor_reduce(amax[:, 0:1], w_row, AX.XY, ALU.max, apply_absolute_value=True).then_inc(amax_ready, 1)
            dve.wait_ge(in_c, 16)
            dve.tensor_reduce(amax[:, 1:2], c_row, AX.XY, ALU.max, apply_absolute_value=True).then_inc(amax_ready, 1)
            dve.wait_ge(amax_all, 1)
            link(dve.tensor_scalar(amaxa[:, 2:3], amaxa[:, 2:3], 1.0, None, ALU.max))
            link(dve.tensor_scalar(amaxa[:, :], amaxa[:, :], 2.0 ** -100, None, ALU.max))
            link(dve.tensor_scalar(pow2[:, :].bitcast(i32), amaxa[:, :].bitcast(i32), 0x7F800000, None, ALU.bitwise_and))
            link(dve.reciprocal(scale[:, :], pow2[:, :]))
            link(dve.tensor_scalar(scale[:, :], scale[:, :], 2.0 ** 14, None, ALU.mult))
            s_w, s_c, s_h = scale[:, 0:1], scale[:, 1:2], scale[:, 2:3]
            link(dve.tensor_tensor(kap[:, 1:2], s_w, s_h, ALU.mult))
            link(dve.reciprocal(kap[:, 0:1], kap[:, 1:2]))
            link(dve.reciprocal(inv[:, 1:2], s_c))
            for n, c in ((2, DT / 2), (3, DT), (4, DT / 6)):
                link(dve.tensor_scalar(kap[:, n:n + 1], inv[:, 1:2], c, None, ALU.mult))
            link(dve.tensor_scalar(negc3[:, :], s_c, -1.0 / 3.0, None, ALU.mult))
            link(dve.tensor_scalar(clampc[:, 0:1], s_c, CLAMP, None, ALU.mult))
            link(dve.tensor_scalar(clampc[:, 1:2], s_c, -CLAMP, None, ALU.mult))
            link(dve.memset(konst[:, :, :], 1.0))
            sums_of = recovery_sums()
            for r in range(4):
                link(dve.tensor_scalar(konst[:, r, :], konst[:, r, :], sums_of[r][5], s_c, ALU.mult, ALU.mult))
            link(dve.tensor_copy(udrive[:, 3, :], konst[:, 3, :]))
            link(dve.memset(scol[:, :], 1.0))
            link(dve.tensor_scalar(scol[:, :], scol[:, :], s_c, None, ALU.mult))
            link(dve.tensor_tensor(bhat[:, :].rearrange("p (k b) -> p k b", b=B),
                                   scol[:, :].rearrange("p (k b) -> p k b", b=B),
                                   fbias[:, :].unsqueeze(2).broadcast_to([P, K, B]), ALU.mult))
            link(dve.tensor_scalar(bias3[:, 3, :], bias3[:, 1, :], kap[:, 1:2], None, ALU.mult))
            cT = condT[:, :, :].rearrange("p k b -> p (k b)")
            dve.tensor_copy(q1[:, :], cT).then_inc(q1_ready, 1)
            link(dve.tensor_copy(h[:, :], cT))
            dve.tensor_scalar(phat[:, :], cT, s_c, None, ALU.mult).then_inc(phat_ready, 1)
            for k in range(K):
                link(dve.tensor_scalar(whh[:, 0, k, :], w_row[:, k, :], s_w, None, ALU.mult))
                ins = dve.scalar_tensor_tensor(whh[:, 1, k, :], w_row[:, k, :], s_w, whh[:, 0, k, :],
                                               ALU.mult, ALU.subtract)
            ins.then_inc(whh_ready, 1)
            for k in range(K):
                dve.wait_ge(cturned, k + 1)
                link(dve.tensor_scalar(cpl[:, 0, k, :], bounce[k], s_c, None, ALU.mult))
                ins = dve.scalar_tensor_tensor(cpl[:, 1, k, :], bounce[k], s_c, cpl[:, 0, k, :],
                                               ALU.mult, ALU.subtract)
            ins.then_inc(cpl_ready, 1)
            for b in range(1, B):
                turn_x(b)
            dve.wait_ge(xT_ready, B * K)
            dve.tensor_copy(gate_base[:, 2 * KB:3 * KB].rearrange("p (k b) -> p k b", b=B),
                            bias3[:, 3, 2 * K:3 * K].unsqueeze(2).broadcast_to([P, K, B])).then_inc(hn_base_ready, 1)
            dve.wait_ge(hn_base_ready, 1)

            h3 = h[:, :].rearrange("p (k b) -> p k b", b=B)

            def h_high(v):
                dve.tensor_scalar(hpart[:, :, 0, :], h3, s_h, None, ALU.mult).then_inc(h_hi, 1)

            def h_low(v):
                dve.wait_ge(h_hi, v)
                dve.scalar_tensor_tensor(hpart[:, :, 1, :], h3, s_h, hpart[:, :, 0, :],
                                         ALU.mult, ALU.subtract).then_inc(h_parts, 1)

            def sum_gates(v):
                dve.wait_ge(gibase_ready, v)
                dve.wait_ge(gate_mm, v)
                dve.tensor_reduce(gates[:, :], pgate[:, :].rearrange("p (s c) -> p c s", c=256)[:, 0:GC, 0:3],
                                  AX.X, ALU.add).then_inc(gate_sum, 1)

            def reset(v):
                dve.wait_ge(rz_ready, v)
                dve.tensor_tensor(gated[:, :], gates[:, 2 * KB:3 * KB], rz[:, 0:KB], ALU.mult).then_inc(gated_ready, 1)

            def argument(v, g):
                dve.wait_ge(gated_ready, v)
                dve.scalar_tensor_tensor(narg[:, :].rearrange("p (k b) -> p k b", b=B),
                                         gated[:, :].rearrange("p (k b) -> p k b", b=B), kap[:, 0:1],
                                         gi[:, :, 2 * K:3 * K, g].rearrange("p b n -> p n b"),
                                         ALU.mult, ALU.add).then_inc(narg_ready, 1)

            def weigh_new(v):
                dve.wait_ge(omz_ready, v)
                dve.wait_ge(cand_ready, v)
                dve.tensor_tensor(wn[:, :], omz[:, :], cand[:, :], ALU.mult).then_inc(wn_ready, 1)

            def new_h(v):
                dve.wait_ge(zh_ready, v)
                dve.wait_ge(wn_ready, v)
                dve.tensor_tensor(h[:, :], wn[:, :], zh[:, :], ALU.add).then_inc(h_ready, 1)

            dve.wait_ge(in_rows, 80)
            for c1, c2, o1, o2 in ((1.0, 0.5, ALU.add, ALU.mult), (D - 1.0, 0.0, ALU.mult, ALU.max), (D - 1.0, None, ALU.min, None)):
                ins = (dve.tensor_scalar(grid, grid, c1, c2, o1, o2) if o2 else dve.tensor_scalar(grid, grid, c1, None, o1))
                link(ins)
            h_high(1)
            h_low(1)
            sum_gates(1)
            reset(1)
            argument(1, 0)
            weigh_new(1)
            new_h(1)
            dve.wait_ge(h_ready, 1)
            h_high(2)
            h_low(2)
            sum_gates(2)
            reset(2)
            argument(2, 1)

            def split_tanh(s, v, ready):
                dve.wait_ge(ready, v)
                dve.scalar_tensor_tensor(tpart[:, :, 1, :], tfull[:, :].rearrange("p (k b) -> p k b", b=B), 1.0,
                                         tpart[:, :, 0, :], ALU.mult, ALU.subtract).then_inc(t_parts[s], 1)

            split_tanh(0, 1, tanh0_ready)

            def window(at, u, s, first=False):
                now, tail, gru = at(u + 1), at(u + 2), at(u + 3)
                if s == 0:
                    if not first:
                        dve.wait_ge(q1raw_ready, at(u))
                        dve.tensor_scalar(q1[:, :], q1raw[:, :], CLAMP, -CLAMP, ALU.min, ALU.max).then_inc(q1_ready, 1)
                        dve.wait_ge(q1_ready, now)
                    dve.tensor_tensor(sq[:, 0, :], q1[:, :], q1[:, :], ALU.mult).then_inc(sq_ready[0], 1)
                    weigh_new(tail)
                    dve.wait_ge(sq_ready[0], now)
                    dve.scalar_tensor_tensor(cub[:, :], sq[:, 0, :], -3.0 * (1 + 1 / STEP[0]), q1[:, :],
                                             ALU.add, ALU.mult).then_inc(cub_ready[0], 1)
                    new_h(tail)
                    dve.wait_ge(drive0_ready, now)
                    dve.wait_ge(cub_ready[0], now)
                    dve.scalar_tensor_tensor(stage_base, cub[:, :], negc3[:, :], drive0[:, :],
                                             ALU.mult, ALU.add).then_inc(base_ready[0], 1)
                    dve.wait_ge(h_ready, tail)
                    h_high(gru)
                    h_low(gru)
                else:
                    dve.wait_ge(sq_ready[s], now)
                    dve.wait_ge(qhat_ready[s], now)
                    dve.scalar_tensor_tensor(cub[:, :], sq[:, s, :], -3.0, qt,
                                             ALU.add, ALU.mult).then_inc(cub_ready[s], 1)
                    if s == 3:
                        sum_gates(gru)
                    dve.wait_ge(sums_ready[s if s == 3 else s - 1], now)
                    dve.wait_ge(cub_ready[s], now)
                    dve.scalar_tensor_tensor(stage_base, cub[:, :], -STEP[s - 1] / 3, sums[:, s - 1, :],
                                             ALU.mult, ALU.add).then_inc(base_ready[s], 1)
                if s == 3:
                    dve.tensor_scalar(phat[:, :], sums[:, 3, :], clampc[:, 0:1], clampc[:, 1:2],
                                      ALU.min, ALU.max).then_inc(phat_ready, 1)
                dve.wait_ge(base_ready[s], now)
                dve.wait_ge(stage_mm[s], now)
                dve.tensor_reduce(qt, pstage[:, :].rearrange("p (s c) -> p c s", c=256)[:, 0:KB, 0:3],
                                  AX.X, ALU.add).then_inc(stage_sum[s], 1)
                if s == 0:
                    dve.tensor_tensor(xT_all[:, at(u), :, :].rearrange("p k b -> p (k b)"), x1keep[:, :], q1[:, :],
                                      ALU.add).then_inc(x2_ready, 1)
                if s == 3:
                    reset(gru)
                    argument(gru, tail)
                split_tanh((s + 1) % 4, now, tanh_ready[s])

            ahead = counts(dve, 0)
            window(ahead, 0, 0, first=True)
            turns = [(u, s) for u in range(UNROLL) for s in range(4)]
            with dve.Fori(0, T - 2 * UNROLL + 1, UNROLL) as t:
                at = counts(dve, t)
                for u, s in turns[1:] + [(UNROLL, 0)]:
                    window(at, u, s)
            ahead = counts(dve, T - UNROLL)
            for u, s in turns[1:]:
                window(ahead, u, s)
            dve.wait_ge(q1raw_ready, T)
            dve.tensor_scalar(q1[:, :], q1raw[:, :], CLAMP, -CLAMP, ALU.min, ALU.max).then_inc(q1_ready, 1)
            dve.wait_ge(q1_ready, T + 1)
            dve.wait_ge(x1keep_ready, T)
            dve.tensor_tensor(xT[:, T - 1, :, :].rearrange("p k b -> p (k b)"), x1keep[:, :], q1[:, :],
                              ALU.add).then_inc(x2_ready, 1)

            dve.wait_ge(x2_ready, T + 1)
            for n in range(BLOCKS):
                dve.tensor_reduce(blk[:, :, :, n], xT[:, n * BLOCK:(n + 1) * BLOCK, :, :].rearrange("p t k b -> p k b t"),
                                  AX.X, ALU.add).then_inc(blk_ready, 1)
            made = [0]

            def then(ins):
                made[0] += 1
                ins.then_inc(l2, 1)
                dve.wait_ge(l2, made[0])

            def rsqrt(rows_n, cols, var_done, root_sem, v, out_ap):
                dve.wait_ge(root_sem, v)
                a, r, w = newton[0:rows_n, 0, 0:cols], newton[0:rows_n, 1, 0:cols], newton[0:rows_n, 2, 0:cols]
                then(dve.reciprocal(r, root[0:rows_n, 0:cols]))
                then(dve.tensor_tensor(w, r, r, ALU.mult))
                then(dve.tensor_tensor(w, w, a, ALU.mult))
                then(dve.tensor_scalar(w, w, -0.5, 1.5, ALU.mult, ALU.add))
                then(dve.tensor_tensor(out_ap, r, w, ALU.mult))

            then(dve.tensor_tensor(keyq[0:NB, :], rms_row[0:NB, :], query_row[0:NB, :], ALU.mult))
            dve.wait_ge(sumsq_ready, 1)
            then(dve.tensor_tensor(scratch[0:NB, :], pwork[0][0:NB, :], keyq[0:NB, :], ALU.mult))
            then(dve.tensor_reduce(dot[:, :], scratch[0:NB, :], AX.X, ALU.add))
            dve.tensor_scalar(newton[0:NB, 0, 0:1], sumsq[:, :], 1.0 / D, L2_EPS, ALU.mult, ALU.add).then_inc(var_ready, 1)
            rsqrt(NB, 1, None, root_ready, 1, newton[0:NB, 1, 1:2])
            dve.tensor_tensor(score[:, :], dot[:, :], newton[0:NB, 1, 1:2], ALU.mult).then_inc(score_ready, 1)
            dve.wait_ge(srow_mm, 1)
            then(dve.tensor_copy(srow[:, 0, :, :].rearrange("p b n -> p (b n)"), pq[0:1, 0:NB]))
            then(dve.tensor_reduce(smax[:, 0, :], srow[:, 0, :, :], AX.X, ALU.max))
            dve.tensor_tensor(srow[:, 1, :, :], srow[:, 0, :, :], smax[:, 0, :].unsqueeze(2).broadcast_to([1, B, BLOCKS]),
                              ALU.subtract).then_inc(sexp_in, 1)
            dve.wait_ge(sexp_ready, 1)
            then(dve.tensor_reduce(smax[:, 1, :], srow[:, 2, :, :], AX.X, ALU.add))
            then(dve.reciprocal(smax[:, 2, :], smax[:, 1, :]))
            dve.tensor_tensor(srow[:, 3, :, :], srow[:, 2, :, :], smax[:, 2, :].unsqueeze(2).broadcast_to([1, B, BLOCKS]),
                              ALU.mult).then_inc(attn_ready, 1)
            dve.wait_ge(attn_mm, 1)
            then(dve.tensor_tensor(weighted[:, :, :, :].rearrange("p k b n -> p k (b n)"),
                                   blk[:, :, :, :].rearrange("p k b n -> p k (b n)"),
                                   pwork[1][:, 0:NB].unsqueeze(1).broadcast_to([P, K, NB]), ALU.mult))
            dve.tensor_reduce(att[:, :, :], weighted[:, :, :, :], AX.X, ALU.add).then_inc(att_ready, 1)

            def turn_to_weights(b):
                for k in range(K):
                    e = b * K + k
                    dve.wait_ge(dist_ready, e + 1)
                    dve.tensor_scalar(spread[:, b, k, :], spread[:, b, k, :], 1.0, 1.0, ALU.min, ALU.subtract).then_inc(spread_ready, 1)

            def moments_of(b):
                if b == 0:
                    dve.wait_ge(mats_ready, 2 * K)
                    dve.wait_ge(proj_mm, 1)
                dve.wait_ge(projb_ready, b + 1)
                for n in range(K):
                    e = b * K + n
                    dve.wait_ge(x2s_ready, e + 1)
                    if b >= 1:
                        dve.wait_ge(normed_ready, e - K + 1)
                    dve.tensor_tensor(ytile[:, n, :], x2s[b % 2][:, n, :], projb[:, b, :], ALU.add).then_inc(y_ready, 1)
                    dve.wait_ge(y_ready, e + 1)
                    then(dve.bn_stats(stats[:, :], ytile[:, n, :]))
                    then(dve.bn_aggr(moments[:, b % 2, n, :], stats[:, :]))

            def scale_of(b):
                dve.tensor_scalar(newton[:, 0, :], moments[:, b % 2, :, 1], L2_EPS, None, ALU.add).then_inc(lnvar_ready, 1)
                rsqrt(P, K, None, lnroot_ready, b + 1, rstd[:, b % 2, :])
                dve.scalar_tensor_tensor(shift[:, b % 2, :], moments[:, b % 2, :, 0], -1.0, rstd[:, b % 2, :],
                                         ALU.mult, ALU.mult).then_inc(rstd_ready, 1)
                dve.wait_ge(rstd_ready, b + 1)

            for b in range(B):
                turn_to_weights(b)
            moments_of(0)
            scale_of(0)
            for b in range(B):
                for n in range(K):
                    e = b * K + n
                    dve.wait_ge(shifted_ready, e + 1)
                    dve.tensor_tensor(x3[:, b % 2, n, :], x3[:, b % 2, n, :], x2s[b % 2][:, n, :], ALU.add).then_inc(x3_ready, 1)
                if b + 1 < B:
                    moments_of(b + 1)
                    scale_of(b + 1)
                for n in range(K):
                    e = b * K + n
                    dve.wait_ge(x3_ready, e + 1)
                    dve.wait_ge(sample_mm, e + 1)
                    dve.tensor_tensor(normed[:, b % 2, n, :], x3[:, b % 2, n, :], pwork[e % 2][:, :],
                                      ALU.subtract).then_inc(final_ready, 1)

        @block.tensor
        def _(pe):
            pe.wait_ge(ident_ready, 1)

            def turn_x(b):
                pe.wait_ge(in_x[b % 2], 16 * (b // 2 + 1))
                for n in range(K):
                    e = b * K + n
                    if e >= 4:
                        pe.wait_ge(xT_ready, e - 3)
                    if b == 1:
                        pe.wait_ge(cpl_ready, 1)
                    for k in range(K):
                        mm = pe.transpose(bounce[e % 4][:, k * P:(k + 1) * P], xrow[:, b % 2, n, k * P:(k + 1) * P],
                                          ident[:, :])
                    mm.then_inc(turned, 1)

            def inputs_of_gates(b):
                pe.wait_ge(xT_ready, K * (b + 1))
                for n in range(G3):
                    e = b * G3 + n
                    if e >= 3:
                        pe.wait_ge(gi_done, e - 2)
                    for k in range(K):
                        mm = pe.matmul(pwork[e % 3][:, :], wih[:, k, n * P:(n + 1) * P], xT[:, 0:T, k, b],
                                       start=(k == 0), stop=(k == K - 1))
                    mm.then_inc(gi_mm, 1)

            pe.wait_ge(in_small, 64)
            pe.transpose(pwork[0][:, 0:NS], small, ident[0:NS, 0:NS]).then_inc(small_turned, 1)
            turn_x(0)
            pe.wait_ge(consts_ready, 1)
            pe.wait_ge(in_wih, 16)
            inputs_of_gates(0)
            pe.wait_ge(in_c, 16)
            for k in range(K):
                pe.wait_ge(xT_ready, k + 1)
                for n in range(K):
                    mm = pe.transpose(bounce[k][:, n * P:(n + 1) * P], c_row[:, n, k * P:(k + 1) * P], ident[:, :])
                mm.then_inc(cturned, 1)
            for b in range(1, B):
                turn_x(b)
                inputs_of_gates(b)

            def gates_mm(n):
                for k in range(K):
                    for w in range(2):
                        mm = pe.matmul(gate3[:, 0:2, n * B:(n + 1) * B], whh[:, w, k, n * P:(n + 1) * P],
                                       hpart[:, k, :, :], start=(n == 0 and k == 0 and w == 0),
                                       stop=(n == G3 - 1 and k == K - 1 and w == 1), skip_group_check=True)
                return mm

            def gates_all(v):
                pe.wait_ge(h_parts, v)
                for n in range(G3):
                    mm = gates_mm(n)
                mm.then_inc(gate_mm, 1)

            pe.wait_ge(whh_ready, 1)
            gates_all(1)
            gates_all(2)

            def step(at, u):
                now, gru = at(u + 1), at(u + 3)
                for s in range(4):
                    pe.wait_ge(t_parts[s], now)
                    for n in range(K):
                        for k in range(K):
                            for w in range(2):
                                mm = pe.matmul(stage3[:, 0:2, n * B:(n + 1) * B], cpl[:, w, k, n * P:(n + 1) * P],
                                               tpart[:, k, :, :], start=(n == 0 and k == 0 and w == 0),
                                               stop=(n == K - 1 and k == K - 1 and w == 1), skip_group_check=True)
                    mm.then_inc(stage_mm[s], 1)
                    if s == 0:
                        pe.wait_ge(h_parts, gru)
                    if s < 3:
                        for n in range(4 * s, 4 * s + 4):
                            mm = gates_mm(n)
                    if s == 2:
                        mm.then_inc(gate_mm, 1)

            with pe.Fori(0, T - UNROLL + 1, UNROLL) as t:
                at = counts(pe, t)
                for u in range(UNROLL):
                    step(at, u)

            pe.wait_ge(in_mats, 32)
            for k in range(2 * K):
                if k == 0:
                    pe.wait_ge(stage_sum[3], T)
                if k >= 4:
                    pe.wait_ge(mats_ready, k - 3)
                for n in range(K):
                    row = wk_row if k < K else wo_row
                    mm = pe.transpose(bounce[k % 4][:, n * P:(n + 1) * P], row[:, n, (k % K) * P:(k % K + 1) * P], ident[:, :])
                mm.then_inc(mats_turned, 1)
            pe.wait_ge(blk_ready, BLOCKS)
            pe.wait_ge(mats_ready, 2 * K)
            for k in range(K):
                mm = pe.matmul(pwork[0][0:NB, :], blk[:, k, :, :].rearrange("p b n -> p (b n)"), wkT[:, k, :],
                               start=(k == 0), stop=(k == K - 1))
            mm.then_inc(keys_mm, 1)
            pe.wait_ge(score_ready, 1)
            pe.matmul(pq[0:1, 0:NB], score[:, :], ident[0:NB, 0:NB], start=True, stop=True).then_inc(srow_mm, 1)
            pe.wait_ge(pick_ready, 2)
            pe.wait_ge(attn_ready, 1)
            pe.matmul(pwork[1][:, 0:NB], onerow[:, :], srow[:, 3, :, :].rearrange("p b n -> p (b n)"),
                      start=True, stop=True).then_inc(attn_mm, 1)
            pe.wait_ge(att_ready, 1)
            for k in range(K):
                mm = pe.matmul(pwork[2][0:B, :], att[:, k, :], woT[:, k, :], start=(k == 0), stop=(k == K - 1))
            mm.then_inc(proj_mm, 1)
            pe.wait_ge(proj4_ready, 1)
            for b in range(B):
                pe.matmul(bounce[b], pick[:, b, :], proj4, start=True, stop=True).then_inc(projb_mm, 1)

            def turn_x2(b):
                for n in range(K):
                    e = b * K + n
                    if e < 2:
                        pe.wait_ge(projb_ready, B)
                    else:
                        pe.wait_ge(x2s_ready, e - 1)
                    for k in range(K):
                        mm = pe.transpose(bounce[e % 2][:, k * P:(k + 1) * P], xT[:, n * P:(n + 1) * P, k, b], ident[:, :])
                    mm.then_inc(x2_turned, 1)

            turn_x2(0)
            for b in range(B):
                if b + 1 < B:
                    turn_x2(b + 1)
                for n in range(K):
                    e = b * K + n
                    pe.wait_ge(x3_ready, e + 1)
                    if e >= 2:
                        pe.wait_ge(x3T_ready, e - 1)
                    for k in range(K):
                        mm = pe.transpose(bounce[2 + e % 2][:, k * P:(k + 1) * P], x3[:, b % 2, n, k * P:(k + 1) * P], ident[:, :])
                    mm.then_inc(x3_turned, 1)
                    pe.wait_ge(x3T_ready, e + 1)
                    if e >= 2:
                        pe.wait_ge(final_ready, e - 1)
                    pe.wait_ge(spread_ready, K * (b + 1))
                    for k in range(K):
                        mm = pe.matmul(pwork[e % 2][:, :], x3T[:, e % 2, k, :], spread[:, b, k, :],
                                       start=(k == 0), stop=(k == K - 1))
                    mm.then_inc(sample_mm, 1)


_INS = ['x', 'cond_2048', 'L0_cond_W_ih', 'L0_cond_W_hh', 'L0_cond_b_ih', 'L0_cond_b_hh', 'L1_cond_coupling',
        'L1_cond_bias', 'L2_cond_rms_weight', 'L2_cond_Wk', 'L2_cond_Wo', 'L2_cond_ln_gamma', 'L2_cond_ln_beta']
_OUTS = [((B, T, D), 'float32')]


def kernel(**inputs):
    import numpy as _np
    import concourse.bacc as _bacc
    from concourse import mybir as _mybir
    from concourse.bass_utils import run_bass_kernel_spmd as _run

    nc = _bacc.Bacc("TRN2", target_bir_lowering=False, num_devices=1)
    arrays, args = {}, []
    for name in _INS:
        a = _np.ascontiguousarray(inputs[name])
        arrays[f"in_{name}_dram"] = a
        args.append(nc.dram_tensor(f"in_{name}_dram", a.shape, _mybir.dt.from_np(a.dtype), kind="ExternalInput").ap())
    for i, (shape, dtype) in enumerate(_OUTS):
        dt = _mybir.dt.from_np(_np.dtype(dtype))
        args.append(nc.dram_tensor(f"out_{i}_dram", shape, dt, kind="ExternalOutput").ap())
    build(nc, *args)
    r = _run(nc, [arrays], core_ids=[0])
    got = tuple(r.results[0][f"out_{i}_dram"] for i in range(len(_OUTS)))
    return got[0]
```

```python
import math

import concourse.bass as bass
from concourse import mybir
from contextlib import ExitStack

fp32 = mybir.dt.float32
fp16 = mybir.dt.float16
i32 = mybir.dt.int32
ALU = mybir.AluOpType
ACT = mybir.ActivationFunctionType
AX = mybir.AxisListType

B, T, D = 4, 512, 512
P = 128
K = D // P
KB = K * B
G3 = 3 * K
GC = G3 * B

DT, EPS, ALPHA, BETA, CLAMP = 0.01, 0.08, 0.7, 0.8, 20.0
STEP = [DT / 2, DT / 2, DT, DT / 6]

BLOCKS, L2_EPS = 8, 1e-6
BLOCK = T // BLOCKS


def recovery_sums():
    def vec(p=0.0, q1=0.0, q2=0.0, q3=0.0, q4=0.0, one=0.0):
        return [p, q1, q2, q3, q4, one]

    def lin(*terms):
        return [sum(c * v[i] for c, v in terms) for i in range(6)]

    p1, one = vec(p=1), vec(one=1)
    q = [vec(q1=1), vec(q2=1), vec(q3=1), vec(q4=1)]

    def slope(qs, ps):
        return lin((EPS, qs), (EPS * ALPHA, one), (-EPS * BETA, ps))

    d1 = slope(q[0], p1)
    p2 = lin((1, p1), (DT / 2, d1))
    d2 = slope(q[1], p2)
    p3 = lin((1, p1), (DT / 2, d2))
    d3 = slope(q[2], p3)
    p4 = lin((1, p1), (DT, d3))
    d4 = slope(q[3], p4)
    pn = lin((1, p1), (DT / 6, d1), (DT / 3, d2), (DT / 3, d3), (DT / 6, d4))
    return [lin((-1, p2), (2 / DT, q[0])),
            lin((-1, p3), (1 / DT, q[0])),
            lin((-1, p4), (-2 / DT, q[0]), (2 / DT, q[1]), (4 / DT, q[2]), (2 / DT, q[3])),
            pn]


UNROLL = 4
HALVES = 2
HK, HC = K // HALVES, KB // HALVES
GATE_ORDER = list(range(2 * K, 3 * K)) + list(range(0, 2 * K))
GATES_AFTER = [range(0, K), range(K, 2 * K), range(2 * K, G3), range(0)]


def counts(eng, first):
    known = {}

    def at(n):
        if isinstance(first, int):
            return first + n
        if n not in known:
            known[n] = eng.snap(first + n)
        return known[n]
    return at


def build(nc, x, cond, W_ih, W_hh, b_ih, b_hh, coupling, fhn_bias, rms_w, Wk, Wo, ln_g, ln_b, out):
    ctx = ExitStack()
    with ctx:
        def sb(name, shape, dt=fp32):
            return ctx.enter_context(nc.sbuf_tensor(name, shape, dt))

        def ps(name, shape, dt=fp32):
            return ctx.enter_context(nc.psum_tensor(name, shape, dt))

        def sem(name):
            return ctx.enter_context(nc.semaphore(name))

        xT_all = sb("xT", [P, T + 2, K, B])
        xT = xT_all[:, 1:T + 1, :, :]
        gi = sb("gi", [P, B, G3, T + 2])
        whh = sb("whh", [P, 2, K, 3 * D], fp16)
        cpl = sb("cpl", [P, 2, K, D], fp16)
        wih = sb("wih", [P, K, 3 * D])
        xrow = sb("xrow", [P, 2, K, D])
        ident = sb("ident", [P, P])
        NS = KB + 2 * G3 + K
        condT = sb("condT", [P, K, B])
        bias3 = sb("bias3", [P, 4, G3])
        fbias = sb("fbias", [P, K])
        amax = sb("amax", [P, 3])
        amaxa = sb("amaxa", [P, 3])
        pow2 = sb("pow2", [P, 3])
        scale = sb("scale", [P, 3])
        sprod = sb("sprod", [P, 1])
        inv = sb("inv", [P, 2])
        kap = sb("kap", [P, 5])
        negc3 = sb("negc3", [P, 1])
        h = sb("h", [P, KB])
        hpart = sb("hpart", [P, K, 2, B], fp16)
        gates = sb("gates", [P, GC])
        rz = sb("rz", [P, 2 * KB])
        gated = sb("gated", [P, KB])
        narg = sb("narg", [P, KB])
        cand = sb("cand", [P, KB])
        hdiff = sb("hdiff", [P, KB])
        zdiff = sb("zdiff", [P, KB])
        q1raw = sb("q1raw", [P, KB])
        q1 = sb("q1", [P, KB])
        tfull = sb("tfull", [P, KB])
        tpart = sb("tpart", [P, 2, K, 2, B], fp16)
        sq = sb("sq", [P, 4, KB])
        sqkept = sb("sqkept", [P, KB])
        cub = sb("cub", [P, KB])
        qhat = sb("qhat", [P, 4, KB])
        phat = sb("phat", [P, KB])
        x1 = sb("x1", [P, KB])
        x1keep = sb("x1keep", [P, KB])
        uscaled = sb("uscaled", [P, KB])
        uhat = sb("uhat", [P, KB])
        drive0 = sb("drive0", [P, KB])
        udrive = sb("udrive", [P, 4, KB])
        psum_p = sb("psum_p", [P, 4, KB])
        sums0 = sb("sums0", [P, 4, KB])
        sums = sb("sums", [P, 4, KB])
        term = sb("term", [P, 4, KB])
        coef = sb("coef", [P, 5, 4, KB])
        konst = sb("konst", [P, 4, KB])
        scol = sb("scol", [P, KB])
        bhat = sb("bhat", [P, KB])
        clampc = sb("clampc", [P, 2])
        ones = sb("ones", [P, KB])

        bank = 512
        psum = ps("psum", [P, 8 * bank])

        def triple(first, stride):
            return psum[:, first:first + 3 * stride].rearrange("p (s c) -> p s c", c=stride)

        half = bank // 2
        stage_base = psum[:, bank:bank + KB]
        stage3 = [triple(0, half), triple(bank + HC, bank - HC)]
        stage_out = [stage3[0][:, 0:2, :], stage3[1][:, 1:3, :]]
        gate_base = psum[:, 4 * bank:4 * bank + GC]
        gate3 = [triple(3 * bank, half), triple(4 * bank + 2 * KB, bank - 2 * KB)]
        gate_out = [gate3[0][:, 0:2, :], gate3[1][:, 1:3, :]]
        qt = psum[:, 6 * bank:8 * bank].rearrange("p (a c) -> p a c", c=bank)[:, :, 0:HC]
        banks = [psum[:, i * bank:(i + 1) * bank] for i in range(8)]
        bounce, pwork, pscore = banks[0:4], banks[5:8], banks[4]

        small = gi[0:NS, 1, 0, 0:P]
        c_row = gi[:, 2, :, :].rearrange("p n t -> p (n t)")[:, 0:K * D].rearrange("p (n k) -> p n k", n=K)
        w_row = gi[:, 3, :, :].rearrange("p n t -> p (n t)")[:, 0:K * 3 * D].rearrange("p (k n) -> p k n", k=K)

        wih_flat = wih[:, :, :].rearrange("p k n -> p (k n)")
        wk_row = wih_flat[:, 0:K * D].rearrange("p (n d) -> p n d", n=K)
        wo_row = wih_flat[:, K * D:2 * K * D].rearrange("p (n d) -> p n d", n=K)
        x3T = wih_flat[:, 0:2 * D].rearrange("p (a k t) -> p a k t", a=2, k=K)
        ytile = wih_flat[:, 2 * D:6 * D].rearrange("p (a d) -> p a d", a=4)
        rows = xrow[:, :, :, :].rearrange("p a n d -> p (a n d)")
        grid = rows[:, 0:B * D].rearrange("p (b d) -> p b d", b=B)
        rms_row, gamma_row, beta_row, query_row = [rows[:, (B + i) * D:(B + i + 1) * D] for i in range(4)]
        space = gi[:, :, :, :].rearrange("p b n t -> p (b n t)")

        def take(at, n):
            return space[:, at * D:(at + n) * D]

        spread = take(0, B * K).rearrange("p (b k l) -> p b k l", b=B, k=K)
        normed = take(16, 8).rearrange("p (a n d) -> p a n d", a=2, n=K)
        x3 = take(24, 8).rearrange("p (a n d) -> p a n d", a=2, n=K)
        projb = take(32, 4).rearrange("p (b d) -> p b d", b=B)
        wkT = take(36, 4).rearrange("p (k n) -> p k n", k=K)
        woT = take(40, 4).rearrange("p (k n) -> p k n", k=K)
        scratch = take(44, 1)
        proj4 = take(45, 1)[0:B, :]
        keyq = take(46, 1)
        x2s_a = whh[:, 0, :, :].rearrange("p k n -> p (k n)").bitcast(fp32)[:, 0:K * D].rearrange("p (n d) -> p n d", n=K)
        x2s_b = whh[:, 1, :, :].rearrange("p k n -> p (k n)").bitcast(fp32)[:, 0:K * D].rearrange("p (n d) -> p n d", n=K)
        x2s = [x2s_a, x2s_b]
        NB = B * BLOCKS
        blk = wih_flat[:, 9 * D + P:9 * D + 2 * P].rearrange("p (k b n) -> p k b n", k=K, b=B)
        weighted = wih_flat[:, 8 * D:8 * D + K * NB].rearrange("p (k b n) -> p k b n", k=K, b=B)
        att = sb("att", [P, K, B])
        feature = sb("feature", [P, K])
        sumsq = sb("sumsq", [NB, 1])
        dot = sb("dot", [NB, 1])
        root = sb("root", [P, 4])
        newton = sb("newton", [P, 3, 4])
        score = sb("score", [NB, 1])
        srow = sb("srow", [1, 5, B, BLOCKS])
        smax = sb("smax", [1, 3, B])
        onerow = wih_flat[0:1, 9 * D:9 * D + P]
        pick = wih_flat[0:B, 10 * D:11 * D].rearrange("p (b m) -> p b m", b=B)
        stats = sb("stats", [P, 6])
        moments = sb("moments", [P, 2, K, 2])
        shift = sb("shift", [P, 2, K])
        rstd = sb("rstd", [P, 2, K])

        hn_base_ready = sem("hn_base_ready")
        small_turned = sem("small_turned")
        in_small, in_wih, in_whh, in_c = sem("in_small"), sem("in_wih"), sem("in_whh"), sem("in_c")
        in_x = [sem(f"in_x{i}") for i in range(2)]
        ident_ready, ident_raw = sem("ident_ready"), sem("ident_raw")
        amax_ready, amax_all, setup = sem("amax_ready"), sem("amax_all"), sem("setup")
        consts_ready = sem("consts_ready")
        turned = sem("turned")
        cturned = sem("cturned")
        gi_mm, gi_done = sem("gi_mm"), sem("gi_done")
        whh_ready = sem("whh_ready")
        xT_ready, cpl_ready, tanh0_ready = sem("xT_ready"), sem("cpl_ready"), sem("tanh0_ready")
        clear_ready = sem("clear_ready")

        h_parts, gibase_ready = sem("h_parts"), sem("gibase_ready")
        nr_mm, z_mm, nr_sum, z_sum = sem("nr_mm"), sem("z_mm"), sem("nr_sum"), sem("z_sum")
        r_ready, z_ready, gated_ready, narg_ready = sem("r_ready"), sem("z_ready"), sem("gated_ready"), sem("narg_ready")
        cand_ready, hdiff_ready, zdiff_ready = sem("cand_ready"), sem("hdiff_ready"), sem("zdiff_ready")
        h_ready, h_hi = sem("h_ready"), sem("h_hi")

        t_parts = [[sem(f"t_parts{s}{a}") for a in "ab"] for s in range(4)]
        stage_mm = [[sem(f"stage_mm{s}{a}") for a in "ab"] for s in range(4)]
        stage_sum = [[sem(f"stage_sum{s}{a}") for a in "ab"] for s in range(4)]
        tanh_ready = [[sem(f"tanh_ready{s}{a}") for a in "ab"] for s in range(4)]
        sq_ready = [sem(f"sq_ready{s}") for s in range(4)]
        qhat_ready = [sem(f"qhat_ready{s}") for s in range(4)]
        cub_ready = [sem(f"cub_ready{s}") for s in range(4)]
        base_ready = [sem(f"base_ready{s}") for s in range(4)]
        term_ready = [sem(f"term_ready{s}") for s in range(4)]
        sums_ready = [sem(f"sums_ready{s}") for s in range(4)]
        q1raw_ready, q1_ready, sqkept_ready = sem("q1raw_ready"), sem("q1_ready"), sem("sqkept_ready")
        x1_ready, uscaled_ready, uhat_ready, udrive_ready = sem("x1_ready"), sem("uscaled_ready"), sem("uhat_ready"), sem("udrive_ready")
        phat_ready, psum_p_ready, sums0_ready = sem("phat_ready"), sem("psum_p_ready"), sem("sums0_ready")
        drive0_ready, x2_ready, x1keep_ready = sem("drive0_ready"), sem("x2_ready"), sem("x1keep_ready")
        out_sem = [sem(f"out_sem{i}") for i in range(2 * K)]
        in_mats, in_rows = sem("in_mats"), sem("in_rows")
        feature_ready, pick_ready = sem("feature_ready"), sem("pick_ready")
        dist_ready, spread_ready = sem("dist_ready"), sem("spread_ready")
        mats_turned, mats_ready = sem("mats_turned"), sem("mats_ready")
        blk_ready, keys_mm, sumsq_ready = sem("blk_ready"), sem("keys_mm"), sem("sumsq_ready")
        score_ready, srow_mm, sexp_in, sexp_ready = sem("score_ready"), sem("srow_mm"), sem("sexp_in"), sem("sexp_ready")
        attn_ready, attn_mm, att_ready = sem("attn_ready"), sem("attn_mm"), sem("att_ready")
        proj_mm, proj4_ready, projb_mm, projb_ready = sem("proj_mm"), sem("proj4_ready"), sem("projb_mm"), sem("projb_ready")
        var_ready, root_ready = sem("var_ready"), sem("root_ready")
        l2 = sem("l2")
        x2_turned, x2s_ready, y_ready = sem("x2_turned"), sem("x2s_ready"), sem("y_ready")
        lnvar_ready, lnroot_ready, rstd_ready = sem("lnvar_ready"), sem("lnroot_ready"), sem("rstd_ready")
        normed_ready, scaled_ready, shifted_ready, x3_ready = sem("normed_ready"), sem("scaled_ready"), sem("shifted_ready"), sem("x3_ready")
        x3_turned, x3T_ready, sample_mm, final_ready = sem("x3_turned"), sem("x3T_ready"), sem("sample_mm"), sem("final_ready")

        block = ctx.enter_context(nc.Block())

        @block.sync
        def _(sp):
            def load_x(b):
                sp.dma_start(xrow[:, b % 2, :, :], x[b].rearrange("(n p) d -> p n d", p=P)).then_inc(in_x[b % 2], 16)

            load_x(0)
            sp.dma_start(w_row, W_hh.rearrange("(k p) n -> p k n", p=P)).then_inc(in_whh, 16)
            sp.dma_start(c_row, coupling.rearrange("(n p) k -> p n k", p=P)).then_inc(in_c, 16)
            sp.dma_start(wih[:, :, :], W_ih.rearrange("(k p) n -> p k n", p=P)).then_inc(in_wih, 16)
            load_x(1)
            for b in range(2, B):
                sp.wait_ge(turned, K * (b - 1))
                load_x(b)
            sp.wait_ge(turned, B * K)
            sp.dma_start(grid.rearrange("p b d -> p (b d)"),
                         cond.rearrange("b d -> (b d)").unsqueeze(0).broadcast_to([P, B * D])).then_inc(in_rows, 16)
            for dst, src in ((rms_row, rms_w), (gamma_row, ln_g), (beta_row, ln_b), (query_row, cond[1])):
                sp.dma_start(dst, src.unsqueeze(0).broadcast_to([P, D])).then_inc(in_rows, 16)
            sp.wait_ge(gi_mm, B * G3)
            sp.dma_start(wk_row, Wk.rearrange("(n p) d -> p n d", p=P)).then_inc(in_mats, 16)
            sp.dma_start(wo_row, Wo.rearrange("(n p) d -> p n d", p=P)).then_inc(in_mats, 16)
            for e in range(B * K):
                sp.wait_ge(final_ready, e + 1)
                sp.dma_start(out[e // K, (e % K) * P:(e % K + 1) * P, :], normed[:, e // K % 2, e % K, :]).then_inc(out_sem[e % (2 * K)], 16)
            for place in range(2 * K):
                sp.wait_ge(out_sem[place], 16 * (B // 2))

        @block.gpsimd
        def _(pool):
            pool.memset(ident[:, :], 0.0).then_inc(ident_raw, 1)
            pool.wait_ge(ident_raw, 1)
            pool.affine_select(out=ident[:, :], in_=ident[:, :], compare_op=ALU.not_equal, fill=1.0, base=0,
                               pattern=[[-1, P]], channel_multiplier=1).then_inc(ident_ready, 1)
            sums_of = recovery_sums()
            for src in range(5):
                for r in range(4):
                    pool.memset(coef[:, src, r, :], sums_of[r][src])
            pool.iota(feature[:, :], pattern=[[-P, K]], base=0, channel_multiplier=-1,
                      allow_small_or_imprecise_dtypes=True).then_inc(feature_ready, 1)
            pool.memset(ones[:, :], 1.0)
            pool.memset(xT_all[:, T + 1, :, :], 0.0)
            pool.memset(x1keep[:, :], 0.0)
            pool.wait_ge(amax_ready, 3)
            pool.partition_all_reduce(amaxa[:, :], amax[:, :], P, bass.bass_isa.ReduceOp.max).then_inc(amax_all, 1)
            pool.wait_ge(phat_ready, 1)

            def next_drive(v, t_next):
                pool.wait_ge(h_ready, v)
                pool.tensor_tensor(x1[:, :], xT_all[:, t_next + 1, :, :].rearrange("p k b -> p (k b)"), h[:, :],
                                   ALU.add).then_inc(x1_ready, 1)
                pool.wait_ge(x1_ready, v)
                pool.tensor_tensor(uscaled[:, :], x1[:, :], scol[:, :], ALU.mult).then_inc(uscaled_ready, 1)
                pool.wait_ge(uscaled_ready, v)
                pool.tensor_tensor(uhat[:, :], uscaled[:, :], bhat[:, :], ALU.add).then_inc(uhat_ready, 1)
                pool.wait_ge(uhat_ready, v)
                pool.tensor_tensor(udrive[:, 0:3, :], konst[:, 0:3, :],
                                   uhat[:, :].unsqueeze(1).broadcast_to([P, 3, KB]), ALU.add).then_inc(udrive_ready, 1)

            def start_sums(v):
                pool.wait_ge(phat_ready, v)
                pool.tensor_tensor(drive0[:, :], uhat[:, :], phat[:, :], ALU.subtract).then_inc(drive0_ready, 1)
                pool.tensor_tensor(psum_p[:, :, :], coef[:, 0, :, :],
                                   phat[:, :].unsqueeze(1).broadcast_to([P, 4, KB]), ALU.mult).then_inc(psum_p_ready, 1)
                pool.wait_ge(psum_p_ready, v)
                pool.tensor_tensor(sums0[:, :, :], psum_p[:, :, :], udrive[:, :, :], ALU.add).then_inc(sums0_ready, 1)

            pool.wait_ge(whh_ready, 1)
            pool.wait_ge(cpl_ready, 1)
            pool.memset(gi[:, :, :, T:T + 2], 0.0).then_inc(clear_ready, 1)
            next_drive(1, 0)
            start_sums(1)

            def step(at, u):
                now, tail = at(u + 1), at(u + 2)
                pool.wait_ge(q1_ready, now)
                pool.tensor_tensor(qhat[:, 0, :], q1[:, :], scol[:, :], ALU.mult).then_inc(qhat_ready[0], 1)
                pool.wait_ge(qhat_ready[0], now)
                pool.tensor_tensor(term[:, :, :], coef[:, 1, :, :],
                                   qhat[:, 0, :].unsqueeze(1).broadcast_to([P, 4, KB]), ALU.mult).then_inc(term_ready[0], 1)
                pool.wait_ge(sums0_ready, now)
                pool.wait_ge(term_ready[0], now)
                pool.tensor_tensor(sums[:, :, :], sums0[:, :, :], term[:, :, :], ALU.add).then_inc(sums_ready[0], 1)
                for s, lo in ((1, 1), (2, 2), (3, 2)):
                    pool.wait_ge(qhat_ready[s], now)
                    pool.wait_ge(sums_ready[s - 1], now)
                    pool.tensor_tensor(term[:, lo:4, :], coef[:, 1 + s, lo:4, :],
                                       qhat[:, s, :].unsqueeze(1).broadcast_to([P, 4 - lo, KB]),
                                       ALU.mult).then_inc(term_ready[s], 1)
                    pool.wait_ge(term_ready[s], now)
                    pool.tensor_tensor(sums[:, lo:4, :], sums[:, lo:4, :], term[:, lo:4, :],
                                       ALU.add).then_inc(sums_ready[s], 1)
                    if s == 1:
                        pool.wait_ge(x2_ready, now)
                        pool.tensor_tensor(x1keep[:, :], x1[:, :], ones[:, :], ALU.mult).then_inc(x1keep_ready, 1)
                        pool.wait_ge(x1keep_ready, now)
                        next_drive(tail, now)
                start_sums(tail)

            with pool.Fori(0, T - UNROLL + 1, UNROLL) as t:
                at = counts(pool, t)
                for u in range(UNROLL):
                    step(at, u)

            pool.wait_ge(gi_mm, B * G3)
            pool.memset(onerow[:, :], 1.0)
            pool.memset(pick[:, :, :], 0.0).then_inc(pick_ready, 1)
            pool.wait_ge(pick_ready, 1)
            pool.affine_select(out=pick[:, :, :], in_=pick[:, :, :], compare_op=ALU.not_equal, fill=1.0, base=0,
                               pattern=[[-1, B], [0, P]], channel_multiplier=1).then_inc(pick_ready, 1)
            for b in range(B):
                for n in range(K):
                    e = b * K + n
                    pool.wait_ge(normed_ready, e + 1)
                    pool.tensor_tensor(x3[:, b % 2, n, :], normed[:, b % 2, n, :], gamma_row, ALU.mult).then_inc(scaled_ready, 1)
                    pool.wait_ge(scaled_ready, e + 1)
                    pool.tensor_tensor(x3[:, b % 2, n, :], x3[:, b % 2, n, :], beta_row, ALU.add).then_inc(shifted_ready, 1)
        @block.scalar
        def _(act):
            for src, at, n in ((cond.rearrange("b (k p) -> (b k) p", p=P), 0, KB),
                               (b_ih.rearrange("(n p) -> n p", p=P), KB, G3),
                               (b_hh.rearrange("(n p) -> n p", p=P), KB + G3, G3),
                               (fhn_bias.rearrange("(n p) -> n p", p=P), KB + 2 * G3, K)):
                act.dma_start(small[at:at + n, :], src).then_inc(in_small, 16)
            act.wait_ge(consts_ready, 1)
            for b in range(B):
                if b == 2:
                    act.wait_ge(cpl_ready, 1)
                if b == 3:
                    act.wait_ge(whh_ready, 1)
                for n in range(G3):
                    e = b * G3 + n
                    act.wait_ge(gi_mm, e + 1)
                    act.activation(gi[:, b, n, 0:T], pwork[e % 3][:, :], ACT.Identity,
                                   bias=bias3[:, 2, n:n + 1]).then_inc(gi_done, 1)
            k_gate, k_prod, k_half, k_full, k_sixth = [act.alloc_register(f"act_scale{i}") for i in range(5)]
            for n, r in enumerate((k_gate, k_prod, k_half, k_full, k_sixth)):
                act.reg_load(r, kap[0:1, n:n + 1].bitcast(i32))
            k_h = act.alloc_register("act_scale_h")
            act.reg_load(k_h, scale[0:1, 2:3].bitcast(i32))
            k_stage = [k_half, k_half, k_full, k_sixth]

            def gate_input(v, g, read):
                if read is not None:
                    act.wait_ge(z_sum, read)
                act.activation(gate_base[:, KB:3 * KB].rearrange("p (n b) -> p n b", b=B),
                               gi[:, :, 0:2 * K, g].rearrange("p b n -> p n b"), ACT.Copy,
                               scale=k_prod).then_inc(gibase_ready, 1)

            def sigmoid_r(v):
                act.wait_ge(nr_sum, v)
                act.activation(rz[:, 0:KB], gates[:, KB:2 * KB], ACT.Sigmoid, scale=k_gate).then_inc(r_ready, 1)

            def sigmoid_z(v):
                act.wait_ge(z_sum, v)
                act.activation(rz[:, KB:2 * KB], gates[:, 2 * KB:3 * KB], ACT.Sigmoid, scale=k_gate).then_inc(z_ready, 1)

            def candidate(v):
                act.wait_ge(narg_ready, v)
                act.activation(cand[:, :], narg[:, :], ACT.Tanh).then_inc(cand_ready, 1)

            def h_high(v, made):
                act.wait_ge(h_ready, made)
                act.activation(hpart[:, :, 0, :], h[:, :].rearrange("p (k b) -> p k b", b=B), ACT.Copy,
                               scale=k_h).then_inc(h_hi, 1)

            act.wait_ge(clear_ready, 1)
            act.wait_ge(hn_base_ready, 1)
            for v in (1, 2):
                gate_input(v, v - 1, v - 1 if v > 1 else None)
                sigmoid_r(v)
                candidate(v)
                sigmoid_z(v)
            first = condT[:, :, :].rearrange("p k b -> p (k b)")
            for a in range(HALVES):
                act.activation(tpart[:, 0, a * HK:(a + 1) * HK, 0, :], condT[:, a * HK:(a + 1) * HK, :], ACT.Tanh)
                act.activation(tfull[:, a * HC:(a + 1) * HC], first[:, a * HC:(a + 1) * HC], ACT.Tanh).then_inc(tanh0_ready, 1)

            def step(at, u):
                now, tail, gru = at(u + 1), at(u + 2), at(u + 3)
                gate_input(gru, tail, tail)
                for s in range(4):
                    for a in range(HALVES):
                        act.wait_ge(stage_sum[s][a], now)
                        act.activation(tpart[:, (s + 1) % 2, a * HK:(a + 1) * HK, 0, :], qt[:, a, :].rearrange("p (k b) -> p k b", b=B),
                                       ACT.Tanh, scale=k_stage[s])
                        act.activation(tfull[:, a * HC:(a + 1) * HC], qt[:, a, :], ACT.Tanh,
                                       scale=k_stage[s]).then_inc(tanh_ready[s][a], 1)
                    if s < 3:
                        act.activation(sq[:, s + 1, :].rearrange("p (a c) -> p a c", a=HALVES), qt, ACT.Square,
                                       scale=k_stage[s]).then_inc(sq_ready[s + 1], 1)
                        act.activation(qhat[:, s + 1, :].rearrange("p (a c) -> p a c", a=HALVES), qt, ACT.Copy,
                                       scale=STEP[s]).then_inc(qhat_ready[s + 1], 1)
                    else:
                        act.activation(q1raw[:, :].rearrange("p (a c) -> p a c", a=HALVES), qt, ACT.Copy,
                                       scale=k_stage[s]).then_inc(q1raw_ready, 1)
                        act.activation(sq[:, 0, :].rearrange("p (a c) -> p a c", a=HALVES), qt, ACT.Square,
                                       scale=k_stage[s]).then_inc(sq_ready[0], 1)
                        h_high(at(u + 4), gru)
                    if s == 1:
                        sigmoid_r(gru)
                    if s == 2:
                        candidate(gru)
                        sigmoid_z(gru)

            with act.Fori(0, T - UNROLL + 1, UNROLL) as t:
                at = counts(act, t)
                for u in range(UNROLL):
                    step(at, u)

            for k in range(2 * K):
                act.wait_ge(mats_turned, k + 1)
                act.activation(wkT[:, k, :] if k < K else woT[:, k - K, :], bounce[k % 4], ACT.Copy).then_inc(mats_ready, 1)
            def distances(b):
                for k in range(K):
                    act.activation(spread[:, b, k, :], grid[:, b, :], ACT.Abs, bias=feature[:, k:k + 1]).then_inc(dist_ready, 1)

            distances(0)
            act.wait_ge(keys_mm, 1)
            act.activation(scratch[0:NB, :], pwork[0][0:NB, :], ACT.Square, accum_out=sumsq[:, :]).then_inc(sumsq_ready, 1)
            act.wait_ge(var_ready, 1)
            act.activation(root[0:NB, 0:1], newton[0:NB, 0, 0:1], ACT.Sqrt).then_inc(root_ready, 1)
            act.wait_ge(sexp_in, 1)
            act.activation(srow[:, 2, :, :], srow[:, 1, :, :], ACT.Exp).then_inc(sexp_ready, 1)
            act.wait_ge(proj_mm, 1)
            act.activation(proj4, pwork[2][0:B, :], ACT.Copy).then_inc(proj4_ready, 1)
            for b in range(B):
                act.wait_ge(projb_mm, b + 1)
                act.activation(projb[:, b, :], bounce[b], ACT.Copy).then_inc(projb_ready, 1)

            def row_out(b, n):
                e = b * K + n
                act.wait_ge(x2_turned, e + 1)
                if b >= 2:
                    act.wait_ge(x3_ready, e - 2 * K + 1)
                act.activation(x2s[b % 2][:, n, :], bounce[e % 2], ACT.Copy).then_inc(x2s_ready, 1)

            def deviation(b):
                act.wait_ge(lnvar_ready, b + 1)
                act.activation(root[:, :], newton[:, 0, :], ACT.Sqrt).then_inc(lnroot_ready, 1)

            def normalize(b, n):
                e = b * K + n
                act.wait_ge(rstd_ready, b + 1)
                if b >= 2:
                    act.wait_ge(out_sem[e % (2 * K)], 16)
                act.activation(normed[:, b % 2, n, :], ytile[:, n, :], ACT.Identity, bias=shift[:, b % 2, n:n + 1],
                               scale=rstd[:, b % 2, n:n + 1]).then_inc(normed_ready, 1)

            for n in range(K):
                row_out(0, n)
            deviation(0)
            for n in range(K):
                normalize(0, n)
                row_out(1, n)
            deviation(1)
            distances(1)
            for b in range(B):
                for n in range(K):
                    e = b * K + n
                    act.wait_ge(x3_turned, e + 1)
                    if e >= 2:
                        act.wait_ge(sample_mm, e - 1)
                    act.activation(x3T[:, e % 2, :, :].rearrange("p k t -> p (k t)"), bounce[2 + e % 2], ACT.Copy).then_inc(x3T_ready, 1)
                    if b + 1 < B:
                        normalize(b + 1, n)
                    if b + 2 < B:
                        row_out(b + 2, n)
                if b + 2 < B:
                    deviation(b + 2)
                    distances(b + 2)

        @block.vector
        def _(dve):
            done = [0]

            def link(ins):
                done[0] += 1
                ins.then_inc(setup, 1)
                dve.wait_ge(setup, done[0])

            def turn_x(b):
                for n in range(K):
                    e = b * K + n
                    dve.wait_ge(turned, e + 1)
                    dve.tensor_copy(xT[:, n * P:(n + 1) * P, :, b].rearrange("p t k -> p k t"),
                                    bounce[e % 4].rearrange("p (k t) -> p k t", k=K)).then_inc(xT_ready, 1)

            dve.wait_ge(small_turned, 1)
            link(dve.tensor_copy(condT[:, :, :].rearrange("p k b -> p b k"),
                                 pwork[0][:, 0:KB].rearrange("p (b k) -> p b k", k=K)))
            link(dve.tensor_copy(bias3[:, 0:2, :].rearrange("p a n -> p (a n)"), pwork[0][:, KB:KB + 2 * G3]))
            link(dve.tensor_copy(fbias[:, :], pwork[0][:, KB + 2 * G3:NS]))
            link(dve.tensor_copy(bias3[:, 2, :], bias3[:, 0, :]))
            dve.tensor_tensor(bias3[:, 2, 0:2 * K], bias3[:, 0, 0:2 * K], bias3[:, 1, 0:2 * K],
                              ALU.add).then_inc(consts_ready, 1)
            dve.tensor_reduce(amax[:, 2:3], condT[:, :, :].rearrange("p k b -> p (k b)"), AX.X, ALU.max,
                              apply_absolute_value=True).then_inc(amax_ready, 1)
            turn_x(0)
            dve.wait_ge(in_whh, 16)
            dve.tensor_reduce(amax[:, 0:1], w_row, AX.XY, ALU.max, apply_absolute_value=True).then_inc(amax_ready, 1)
            dve.wait_ge(in_c, 16)
            dve.tensor_reduce(amax[:, 1:2], c_row, AX.XY, ALU.max, apply_absolute_value=True).then_inc(amax_ready, 1)
            dve.wait_ge(amax_all, 1)
            link(dve.tensor_scalar(amaxa[:, 2:3], amaxa[:, 2:3], 1.0, None, ALU.max))
            link(dve.tensor_scalar(amaxa[:, :], amaxa[:, :], 2.0 ** -100, None, ALU.max))
            link(dve.tensor_scalar(pow2[:, :].bitcast(i32), amaxa[:, :].bitcast(i32), 0x7F800000, None, ALU.bitwise_and))
            link(dve.reciprocal(scale[:, :], pow2[:, :]))
            link(dve.tensor_scalar(scale[:, :], scale[:, :], 2.0 ** 14, None, ALU.mult))
            s_w, s_c, s_h = scale[:, 0:1], scale[:, 1:2], scale[:, 2:3]
            link(dve.tensor_tensor(kap[:, 1:2], s_w, s_h, ALU.mult))
            link(dve.reciprocal(kap[:, 0:1], kap[:, 1:2]))
            link(dve.reciprocal(inv[:, 1:2], s_c))
            for n, c in ((2, DT / 2), (3, DT), (4, DT / 6)):
                link(dve.tensor_scalar(kap[:, n:n + 1], inv[:, 1:2], c, None, ALU.mult))
            link(dve.tensor_scalar(negc3[:, :], s_c, -1.0 / 3.0, None, ALU.mult))
            link(dve.tensor_scalar(clampc[:, 0:1], s_c, CLAMP, None, ALU.mult))
            link(dve.tensor_scalar(clampc[:, 1:2], s_c, -CLAMP, None, ALU.mult))
            link(dve.memset(konst[:, :, :], 1.0))
            sums_of = recovery_sums()
            for r in range(4):
                link(dve.tensor_scalar(konst[:, r, :], konst[:, r, :], sums_of[r][5], s_c, ALU.mult, ALU.mult))
            link(dve.tensor_copy(udrive[:, 3, :], konst[:, 3, :]))
            link(dve.memset(scol[:, :], 1.0))
            link(dve.tensor_scalar(scol[:, :], scol[:, :], s_c, None, ALU.mult))
            link(dve.tensor_tensor(bhat[:, :].rearrange("p (k b) -> p k b", b=B),
                                   scol[:, :].rearrange("p (k b) -> p k b", b=B),
                                   fbias[:, :].unsqueeze(2).broadcast_to([P, K, B]), ALU.mult))
            link(dve.tensor_scalar(bias3[:, 3, :], bias3[:, 1, :], kap[:, 1:2], None, ALU.mult))
            cT = condT[:, :, :].rearrange("p k b -> p (k b)")
            dve.tensor_copy(q1[:, :], cT).then_inc(q1_ready, 1)
            link(dve.tensor_copy(h[:, :], cT))
            dve.tensor_scalar(phat[:, :], cT, s_c, None, ALU.mult).then_inc(phat_ready, 1)
            for k in range(K):
                link(dve.tensor_scalar(whh[:, 0, k, :], w_row[:, k, :], s_w, None, ALU.mult))
                ins = dve.scalar_tensor_tensor(whh[:, 1, k, :], w_row[:, k, :], s_w, whh[:, 0, k, :],
                                               ALU.mult, ALU.subtract)
            ins.then_inc(whh_ready, 1)
            for k in range(K):
                dve.wait_ge(cturned, k + 1)
                link(dve.tensor_scalar(cpl[:, 0, k, :], bounce[k], s_c, None, ALU.mult))
                ins = dve.scalar_tensor_tensor(cpl[:, 1, k, :], bounce[k], s_c, cpl[:, 0, k, :],
                                               ALU.mult, ALU.subtract)
            ins.then_inc(cpl_ready, 1)
            for b in range(1, B):
                turn_x(b)
            dve.wait_ge(xT_ready, B * K)
            dve.tensor_copy(gate_base[:, 0:KB].rearrange("p (k b) -> p k b", b=B),
                            bias3[:, 3, 2 * K:3 * K].unsqueeze(2).broadcast_to([P, K, B])).then_inc(hn_base_ready, 1)
            dve.wait_ge(hn_base_ready, 1)

            h3 = h[:, :].rearrange("p (k b) -> p k b", b=B)

            def h_high(v):
                dve.tensor_scalar(hpart[:, :, 0, :], h3, s_h, None, ALU.mult).then_inc(h_hi, 1)

            def h_low(v):
                dve.wait_ge(h_hi, v)
                dve.scalar_tensor_tensor(hpart[:, :, 1, :], h3, s_h, hpart[:, :, 0, :],
                                         ALU.mult, ALU.subtract).then_inc(h_parts, 1)

            def sum_nr(v):
                dve.wait_ge(gibase_ready, v)
                dve.wait_ge(nr_mm, v)
                dve.tensor_reduce(gates[:, 0:2 * KB], gate3[0].rearrange("p s c -> p c s")[:, 0:2 * KB, :],
                                  AX.X, ALU.add).then_inc(nr_sum, 1)

            def sum_z(v):
                dve.wait_ge(z_mm, v)
                dve.tensor_reduce(gates[:, 2 * KB:3 * KB], gate3[1].rearrange("p s c -> p c s")[:, 0:KB, :],
                                  AX.X, ALU.add).then_inc(z_sum, 1)

            def reset(v):
                dve.wait_ge(r_ready, v)
                dve.tensor_tensor(gated[:, :], gates[:, 0:KB], rz[:, 0:KB], ALU.mult).then_inc(gated_ready, 1)

            def argument(v, g):
                dve.wait_ge(gated_ready, v)
                dve.scalar_tensor_tensor(narg[:, :].rearrange("p (k b) -> p k b", b=B),
                                         gated[:, :].rearrange("p (k b) -> p k b", b=B), kap[:, 0:1],
                                         gi[:, :, 2 * K:3 * K, g].rearrange("p b n -> p n b"),
                                         ALU.mult, ALU.add).then_inc(narg_ready, 1)

            def difference(v):
                dve.wait_ge(cand_ready, v)
                dve.tensor_tensor(hdiff[:, :], h[:, :], cand[:, :], ALU.subtract).then_inc(hdiff_ready, 1)

            def weigh(v):
                dve.wait_ge(hdiff_ready, v)
                dve.wait_ge(z_ready, v)
                dve.tensor_tensor(zdiff[:, :], rz[:, KB:2 * KB], hdiff[:, :], ALU.mult).then_inc(zdiff_ready, 1)

            def new_h(v, read=None):
                if read is not None:
                    dve.wait_ge(x1_ready, read)
                dve.wait_ge(zdiff_ready, v)
                dve.tensor_tensor(h[:, :], zdiff[:, :], cand[:, :], ALU.add).then_inc(h_ready, 1)

            dve.wait_ge(in_rows, 80)
            for c1, c2, o1, o2 in ((1.0, 0.5, ALU.add, ALU.mult), (D - 1.0, 0.0, ALU.mult, ALU.max), (D - 1.0, None, ALU.min, None)):
                ins = (dve.tensor_scalar(grid, grid, c1, c2, o1, o2) if o2 else dve.tensor_scalar(grid, grid, c1, None, o1))
                link(ins)
            for v in (1, 2):
                h_high(v)
                h_low(v)
                sum_nr(v)
                reset(v)
                argument(v, v - 1)
                difference(v)
                sum_z(v)
                weigh(v)
                new_h(v, v - 1 if v > 1 else None)
                dve.wait_ge(h_ready, v)
            dve.tensor_tensor(sq[:, 0, :], q1[:, :], q1[:, :], ALU.mult).then_inc(sq_ready[0], 1)
            h_high(3)
            h_low(3)

            def split_tanh(s, a, v, ready, n):
                dve.wait_ge(ready, n)
                dve.scalar_tensor_tensor(tpart[:, s % 2, a * HK:(a + 1) * HK, 1, :],
                                         tfull[:, a * HC:(a + 1) * HC].rearrange("p (k b) -> p k b", b=B), 1.0,
                                         tpart[:, s % 2, a * HK:(a + 1) * HK, 0, :], ALU.mult, ALU.subtract).then_inc(t_parts[s][a], 1)

            for a in range(HALVES):
                split_tanh(0, a, 1, tanh0_ready, a + 1)

            def window(at, u, s, first=False):
                now, tail, gru = at(u + 1), at(u + 2), at(u + 3)
                if s == 0:
                    if not first:
                        dve.wait_ge(q1raw_ready, at(u))
                        dve.tensor_scalar(q1[:, :], q1raw[:, :], CLAMP, -CLAMP, ALU.min, ALU.max).then_inc(q1_ready, 1)
                    dve.wait_ge(sq_ready[0], now)
                    dve.tensor_scalar(sqkept[:, :], sq[:, 0, :], CLAMP * CLAMP, -3.0 * (1 + 1 / STEP[0]),
                                      ALU.min, ALU.add).then_inc(sqkept_ready, 1)
                    if not first:
                        h_low(gru)
                    dve.wait_ge(drive0_ready, now)
                    dve.wait_ge(sqkept_ready, now)
                    dve.tensor_tensor(cub[:, :], sqkept[:, :], q1[:, :], ALU.mult).then_inc(cub_ready[0], 1)
                    dve.wait_ge(cub_ready[0], now)
                    dve.scalar_tensor_tensor(stage_base, cub[:, :], negc3[:, :], drive0[:, :],
                                             ALU.mult, ALU.add).then_inc(base_ready[0], 1)
                else:
                    dve.wait_ge(qhat_ready[s], now)
                    dve.scalar_tensor_tensor(cub[:, :].rearrange("p (a c) -> p a c", a=HALVES),
                                             sq[:, s, :].rearrange("p (a c) -> p a c", a=HALVES), -3.0, qt,
                                             ALU.add, ALU.mult).then_inc(cub_ready[s], 1)
                    if s == 3:
                        difference(gru)
                    dve.wait_ge(sums_ready[s if s == 3 else s - 1], now)
                    dve.wait_ge(cub_ready[s], now)
                    dve.scalar_tensor_tensor(stage_base, cub[:, :], -STEP[s - 1] / 3, sums[:, s - 1, :],
                                             ALU.mult, ALU.add).then_inc(base_ready[s], 1)
                    if s == 2:
                        sum_nr(gru)
                    if s == 3:
                        sum_z(gru)
                dve.wait_ge(base_ready[s], now)
                for a in range(HALVES):
                    dve.wait_ge(stage_mm[s][a], now)
                    dve.tensor_reduce(qt[:, a, :], stage3[a].rearrange("p s c -> p c s")[:, 0:HC, :],
                                      AX.X, ALU.add).then_inc(stage_sum[s][a], 1)
                    if s == 3 and a == 0:
                        dve.tensor_scalar(phat[:, :], sums[:, 3, :], clampc[:, 0:1], clampc[:, 1:2],
                                          ALU.min, ALU.max).then_inc(phat_ready, 1)
                if s == 0:
                    dve.tensor_tensor(xT_all[:, at(u), :, :].rearrange("p k b -> p (k b)"), x1keep[:, :], q1[:, :],
                                      ALU.add).then_inc(x2_ready, 1)
                if s == 2:
                    reset(gru)
                if s == 3:
                    weigh(gru)
                split_tanh((s + 1) % 4, 0, now, tanh_ready[s][0], now)
                if s == 2:
                    argument(gru, tail)
                if s == 3:
                    new_h(gru)
                split_tanh((s + 1) % 4, 1, now, tanh_ready[s][1], now)

            ahead = counts(dve, 0)
            window(ahead, 0, 0, first=True)
            turns = [(u, s) for u in range(UNROLL) for s in range(4)]
            with dve.Fori(0, T - 2 * UNROLL + 1, UNROLL) as t:
                at = counts(dve, t)
                for u, s in turns[1:] + [(UNROLL, 0)]:
                    window(at, u, s)
            ahead = counts(dve, T - UNROLL)
            for u, s in turns[1:]:
                window(ahead, u, s)
            dve.wait_ge(q1raw_ready, T)
            dve.tensor_scalar(q1[:, :], q1raw[:, :], CLAMP, -CLAMP, ALU.min, ALU.max).then_inc(q1_ready, 1)
            dve.wait_ge(q1_ready, T + 1)
            dve.wait_ge(x1keep_ready, T)
            dve.tensor_tensor(xT[:, T - 1, :, :].rearrange("p k b -> p (k b)"), x1keep[:, :], q1[:, :],
                              ALU.add).then_inc(x2_ready, 1)

            dve.wait_ge(x2_ready, T + 1)
            for n in range(BLOCKS):
                dve.tensor_reduce(blk[:, :, :, n], xT[:, n * BLOCK:(n + 1) * BLOCK, :, :].rearrange("p t k b -> p k b t"),
                                  AX.X, ALU.add).then_inc(blk_ready, 1)
            made = [0]

            def then(ins):
                made[0] += 1
                ins.then_inc(l2, 1)
                dve.wait_ge(l2, made[0])

            def rsqrt(rows_n, cols, var_done, root_sem, v, out_ap):
                dve.wait_ge(root_sem, v)
                a, r, w = newton[0:rows_n, 0, 0:cols], newton[0:rows_n, 1, 0:cols], newton[0:rows_n, 2, 0:cols]
                then(dve.reciprocal(r, root[0:rows_n, 0:cols]))
                then(dve.tensor_tensor(w, r, r, ALU.mult))
                then(dve.tensor_tensor(w, w, a, ALU.mult))
                then(dve.tensor_scalar(w, w, -0.5, 1.5, ALU.mult, ALU.add))
                then(dve.tensor_tensor(out_ap, r, w, ALU.mult))

            then(dve.tensor_tensor(keyq[0:NB, :], rms_row[0:NB, :], query_row[0:NB, :], ALU.mult))
            dve.wait_ge(sumsq_ready, 1)
            then(dve.tensor_tensor(scratch[0:NB, :], pwork[0][0:NB, :], keyq[0:NB, :], ALU.mult))
            then(dve.tensor_reduce(dot[:, :], scratch[0:NB, :], AX.X, ALU.add))
            dve.tensor_scalar(newton[0:NB, 0, 0:1], sumsq[:, :], 1.0 / D, L2_EPS, ALU.mult, ALU.add).then_inc(var_ready, 1)
            rsqrt(NB, 1, None, root_ready, 1, newton[0:NB, 1, 1:2])
            dve.tensor_tensor(score[:, :], dot[:, :], newton[0:NB, 1, 1:2], ALU.mult).then_inc(score_ready, 1)
            dve.wait_ge(srow_mm, 1)
            then(dve.tensor_copy(srow[:, 0, :, :].rearrange("p b n -> p (b n)"), pscore[0:1, 0:NB]))
            then(dve.tensor_reduce(smax[:, 0, :], srow[:, 0, :, :], AX.X, ALU.max))
            dve.tensor_tensor(srow[:, 1, :, :], srow[:, 0, :, :], smax[:, 0, :].unsqueeze(2).broadcast_to([1, B, BLOCKS]),
                              ALU.subtract).then_inc(sexp_in, 1)
            dve.wait_ge(sexp_ready, 1)
            then(dve.tensor_reduce(smax[:, 1, :], srow[:, 2, :, :], AX.X, ALU.add))
            then(dve.reciprocal(smax[:, 2, :], smax[:, 1, :]))
            dve.tensor_tensor(srow[:, 3, :, :], srow[:, 2, :, :], smax[:, 2, :].unsqueeze(2).broadcast_to([1, B, BLOCKS]),
                              ALU.mult).then_inc(attn_ready, 1)
            dve.wait_ge(attn_mm, 1)
            then(dve.tensor_tensor(weighted[:, :, :, :].rearrange("p k b n -> p k (b n)"),
                                   blk[:, :, :, :].rearrange("p k b n -> p k (b n)"),
                                   pwork[1][:, 0:NB].unsqueeze(1).broadcast_to([P, K, NB]), ALU.mult))
            dve.tensor_reduce(att[:, :, :], weighted[:, :, :, :], AX.X, ALU.add).then_inc(att_ready, 1)

            def turn_to_weights(b):
                for k in range(K):
                    e = b * K + k
                    dve.wait_ge(dist_ready, e + 1)
                    dve.tensor_scalar(spread[:, b, k, :], spread[:, b, k, :], 1.0, 1.0, ALU.min, ALU.subtract).then_inc(spread_ready, 1)

            def moments_of(b, n):
                e = b * K + n
                dve.wait_ge(projb_ready, b + 1)
                dve.wait_ge(x2s_ready, e + 1)
                if b >= 1:
                    dve.wait_ge(normed_ready, e - K + 1)
                dve.tensor_tensor(ytile[:, n, :], x2s[b % 2][:, n, :], projb[:, b, :], ALU.add).then_inc(y_ready, 1)
                dve.wait_ge(y_ready, e + 1)
                then(dve.bn_stats(stats[:, :], ytile[:, n, :]))
                then(dve.bn_aggr(moments[:, b % 2, n, :], stats[:, :]))

            def scale_of(b):
                dve.tensor_scalar(newton[:, 0, :], moments[:, b % 2, :, 1], L2_EPS, None, ALU.add).then_inc(lnvar_ready, 1)
                rsqrt(P, K, None, lnroot_ready, b + 1, rstd[:, b % 2, :])
                dve.scalar_tensor_tensor(shift[:, b % 2, :], moments[:, b % 2, :, 0], -1.0, rstd[:, b % 2, :],
                                         ALU.mult, ALU.mult).then_inc(rstd_ready, 1)
                dve.wait_ge(rstd_ready, b + 1)

            def add_x2(b, n):
                e = b * K + n
                dve.wait_ge(shifted_ready, e + 1)
                dve.tensor_tensor(x3[:, b % 2, n, :], x3[:, b % 2, n, :], x2s[b % 2][:, n, :], ALU.add).then_inc(x3_ready, 1)

            turn_to_weights(0)
            dve.wait_ge(mats_ready, 2 * K)
            dve.wait_ge(proj_mm, 1)
            for n in range(K):
                moments_of(0, n)
            scale_of(0)
            for n in range(K):
                moments_of(1, n)
                add_x2(0, n)
            scale_of(1)
            turn_to_weights(1)
            for b in range(B):
                for n in range(K):
                    e = b * K + n
                    if b + 1 < B:
                        add_x2(b + 1, n)
                    if b + 2 < B:
                        moments_of(b + 2, n)
                    dve.wait_ge(x3_ready, e + 1)
                    dve.wait_ge(sample_mm, e + 1)
                    dve.tensor_tensor(normed[:, b % 2, n, :], x3[:, b % 2, n, :], pwork[e % 2][:, :],
                                      ALU.subtract).then_inc(final_ready, 1)
                if b + 2 < B:
                    scale_of(b + 2)
                    turn_to_weights(b + 2)

        @block.tensor
        def _(pe):
            pe.wait_ge(ident_ready, 1)

            def turn_x(b):
                pe.wait_ge(in_x[b % 2], 16 * (b // 2 + 1))
                for n in range(K):
                    e = b * K + n
                    if e >= 4:
                        pe.wait_ge(xT_ready, e - 3)
                    if b == 1:
                        pe.wait_ge(cpl_ready, 1)
                    for k in range(K):
                        mm = pe.transpose(bounce[e % 4][:, k * P:(k + 1) * P], xrow[:, b % 2, n, k * P:(k + 1) * P],
                                          ident[:, :])
                    mm.then_inc(turned, 1)

            def inputs_of_gates(b):
                pe.wait_ge(xT_ready, K * (b + 1))
                for n in range(G3):
                    e = b * G3 + n
                    if e >= 3:
                        pe.wait_ge(gi_done, e - 2)
                    for k in range(K):
                        mm = pe.matmul(pwork[e % 3][:, :], wih[:, k, n * P:(n + 1) * P], xT[:, 0:T, k, b],
                                       start=(k == 0), stop=(k == K - 1))
                    mm.then_inc(gi_mm, 1)

            pe.wait_ge(in_small, 64)
            pe.transpose(pwork[0][:, 0:NS], small, ident[0:NS, 0:NS]).then_inc(small_turned, 1)
            turn_x(0)
            pe.wait_ge(consts_ready, 1)
            pe.wait_ge(in_wih, 16)
            inputs_of_gates(0)
            pe.wait_ge(in_c, 16)
            for k in range(K):
                pe.wait_ge(xT_ready, k + 1)
                for n in range(K):
                    mm = pe.transpose(bounce[k][:, n * P:(n + 1) * P], c_row[:, n, k * P:(k + 1) * P], ident[:, :])
                mm.then_inc(cturned, 1)
            for b in range(1, B):
                turn_x(b)
                inputs_of_gates(b)

            def gates_mm(c):
                n = GATE_ORDER[c]
                part, col, last = (0, c * B, 2 * K - 1) if c < 2 * K else (1, (c - 2 * K) * B, G3 - 1)
                for k in range(K):
                    for w in range(2):
                        mm = pe.matmul(gate_out[part][:, :, col:col + B], whh[:, w, k, n * P:(n + 1) * P],
                                       hpart[:, k, :, :], start=(col == 0 and k == 0 and w == 0),
                                       stop=(c == last and k == K - 1 and w == 1), skip_group_check=True)
                if c == 2 * K - 1:
                    mm.then_inc(nr_mm, 1)
                if c == G3 - 1:
                    mm.then_inc(z_mm, 1)

            pe.wait_ge(whh_ready, 1)
            pe.wait_ge(gi_done, B * G3)
            for v in (1, 2):
                pe.wait_ge(h_parts, v)
                for c in range(G3):
                    gates_mm(c)

            def stage_products(s, ks, ns):
                for n in ns:
                    a, col = n // HK, n % HK * B
                    for k in ks:
                        for w in range(2):
                            mm = pe.matmul(stage_out[a][:, :, col:col + B], cpl[:, w, k, n * P:(n + 1) * P],
                                           tpart[:, s % 2, k, :, :], start=(col == 0 and k == 0 and w == 0),
                                           stop=(n % HK == HK - 1 and k == K - 1 and w == 1), skip_group_check=True)
                return mm

            k_first, k_second = range(HK), range(HK, K)

            def step(at, u):
                now, tail, gru = at(u + 1), at(u + 2), at(u + 3)
                for s in range(4):
                    pe.wait_ge(t_parts[s][0], now)
                    stage_products(s, k_first, range(HK + 1))
                    pe.wait_ge(t_parts[s][1], now)
                    stage_products(s, k_second, range(HK)).then_inc(stage_mm[s][0], 1)
                    stage_products(s, k_first, range(HK + 1, K))
                    stage_products(s, k_second, range(HK, K)).then_inc(stage_mm[s][1], 1)
                    if s == 0:
                        pe.wait_ge(h_parts, gru)
                    for c in GATES_AFTER[s]:
                        gates_mm(c)

            with pe.Fori(0, T - UNROLL + 1, UNROLL) as t:
                at = counts(pe, t)
                for u in range(UNROLL):
                    step(at, u)

            pe.wait_ge(in_mats, 32)
            for k in range(2 * K):
                if k == 0:
                    pe.wait_ge(stage_sum[3][1], T)
                if k >= 4:
                    pe.wait_ge(mats_ready, k - 3)
                for n in range(K):
                    row = wk_row if k < K else wo_row
                    mm = pe.transpose(bounce[k % 4][:, n * P:(n + 1) * P], row[:, n, (k % K) * P:(k % K + 1) * P], ident[:, :])
                mm.then_inc(mats_turned, 1)
            pe.wait_ge(blk_ready, BLOCKS)
            pe.wait_ge(mats_ready, 2 * K)
            for k in range(K):
                mm = pe.matmul(pwork[0][0:NB, :], blk[:, k, :, :].rearrange("p b n -> p (b n)"), wkT[:, k, :],
                               start=(k == 0), stop=(k == K - 1))
            mm.then_inc(keys_mm, 1)
            pe.wait_ge(score_ready, 1)
            pe.matmul(pscore[0:1, 0:NB], score[:, :], ident[0:NB, 0:NB], start=True, stop=True).then_inc(srow_mm, 1)
            pe.wait_ge(pick_ready, 2)
            pe.wait_ge(attn_ready, 1)
            pe.matmul(pwork[1][:, 0:NB], onerow[:, :], srow[:, 3, :, :].rearrange("p b n -> p (b n)"),
                      start=True, stop=True).then_inc(attn_mm, 1)
            pe.wait_ge(att_ready, 1)
            for k in range(K):
                mm = pe.matmul(pwork[2][0:B, :], att[:, k, :], woT[:, k, :], start=(k == 0), stop=(k == K - 1))
            mm.then_inc(proj_mm, 1)
            pe.wait_ge(proj4_ready, 1)
            for b in range(B):
                pe.matmul(bounce[b], pick[:, b, :], proj4, start=True, stop=True).then_inc(projb_mm, 1)

            def turn_x2(b, n):
                e = b * K + n
                if e < 2:
                    pe.wait_ge(projb_ready, B)
                else:
                    pe.wait_ge(x2s_ready, e - 1)
                for k in range(K):
                    mm = pe.transpose(bounce[e % 2][:, k * P:(k + 1) * P], xT[:, n * P:(n + 1) * P, k, b], ident[:, :])
                mm.then_inc(x2_turned, 1)

            def turn_x3(e):
                b, n = divmod(e, K)
                pe.wait_ge(x3_ready, e + 1)
                if e >= 2:
                    pe.wait_ge(x3T_ready, e - 1)
                for k in range(K):
                    mm = pe.transpose(bounce[2 + e % 2][:, k * P:(k + 1) * P], x3[:, b % 2, n, k * P:(k + 1) * P], ident[:, :])
                mm.then_inc(x3_turned, 1)

            for b in range(2):
                for n in range(K):
                    turn_x2(b, n)
            turn_x3(0)
            for e in range(B * K):
                b, n = divmod(e, K)
                if n < K - 1:
                    turn_x3(e + 1)
                if b + 2 < B:
                    turn_x2(b + 2, n)
                pe.wait_ge(x3T_ready, e + 1)
                if e >= 2:
                    pe.wait_ge(final_ready, e - 1)
                pe.wait_ge(spread_ready, K * (b + 1))
                for k in range(K):
                    mm = pe.matmul(pwork[e % 2][:, :], x3T[:, e % 2, k, :], spread[:, b, k, :],
                                   start=(k == 0), stop=(k == K - 1))
                mm.then_inc(sample_mm, 1)
                if n == K - 1 and b + 1 < B:
                    turn_x3(e + 1)


_INS = ['x', 'cond_2048', 'L0_cond_W_ih', 'L0_cond_W_hh', 'L0_cond_b_ih', 'L0_cond_b_hh', 'L1_cond_coupling',
        'L1_cond_bias', 'L2_cond_rms_weight', 'L2_cond_Wk', 'L2_cond_Wo', 'L2_cond_ln_gamma', 'L2_cond_ln_beta']
_OUTS = [((B, T, D), 'float32')]


def kernel(**inputs):
    import numpy as _np
    import concourse.bacc as _bacc
    from concourse import mybir as _mybir
    from concourse.bass_utils import run_bass_kernel_spmd as _run

    nc = _bacc.Bacc("TRN2", target_bir_lowering=False, num_devices=1)
    arrays, args = {}, []
    for name in _INS:
        a = _np.ascontiguousarray(inputs[name])
        arrays[f"in_{name}_dram"] = a
        args.append(nc.dram_tensor(f"in_{name}_dram", a.shape, _mybir.dt.from_np(a.dtype), kind="ExternalInput").ap())
    for i, (shape, dtype) in enumerate(_OUTS):
        dt = _mybir.dt.from_np(_np.dtype(dtype))
        args.append(nc.dram_tensor(f"out_{i}_dram", shape, dt, kind="ExternalOutput").ap())
    build(nc, *args)
    r = _run(nc, [arrays], core_ids=[0])
    got = tuple(r.results[0][f"out_{i}_dram"] for i in range(len(_OUTS)))
    return got[0]
```

```python
import math

import concourse.bass as bass
from concourse import mybir
from contextlib import ExitStack

fp32 = mybir.dt.float32
fp16 = mybir.dt.float16
i32 = mybir.dt.int32
ALU = mybir.AluOpType
ACT = mybir.ActivationFunctionType
AX = mybir.AxisListType

B, T, D = 4, 512, 512
P = 128
K = D // P
KB = K * B
G3 = 3 * K
GC = G3 * B

DT, EPS, ALPHA, BETA, CLAMP = 0.01, 0.08, 0.7, 0.8, 20.0
STEP = [DT / 2, DT / 2, DT, DT / 6]

BLOCKS, L2_EPS = 8, 1e-6
BLOCK = T // BLOCKS


def recovery_sums():
    def vec(p=0.0, q1=0.0, q2=0.0, q3=0.0, q4=0.0, one=0.0):
        return [p, q1, q2, q3, q4, one]

    def lin(*terms):
        return [sum(c * v[i] for c, v in terms) for i in range(6)]

    p1, one = vec(p=1), vec(one=1)
    q = [vec(q1=1), vec(q2=1), vec(q3=1), vec(q4=1)]

    def slope(qs, ps):
        return lin((EPS, qs), (EPS * ALPHA, one), (-EPS * BETA, ps))

    d1 = slope(q[0], p1)
    p2 = lin((1, p1), (DT / 2, d1))
    d2 = slope(q[1], p2)
    p3 = lin((1, p1), (DT / 2, d2))
    d3 = slope(q[2], p3)
    p4 = lin((1, p1), (DT, d3))
    d4 = slope(q[3], p4)
    pn = lin((1, p1), (DT / 6, d1), (DT / 3, d2), (DT / 3, d3), (DT / 6, d4))
    return [lin((-1, p2), (2 / DT, q[0])),
            lin((-1, p3), (1 / DT, q[0])),
            lin((-1, p4), (-2 / DT, q[0]), (2 / DT, q[1]), (4 / DT, q[2]), (2 / DT, q[3])),
            pn]


UNROLL = 4
HALVES = 2
HK, HC = K // HALVES, KB // HALVES
GATE_ORDER = list(range(2 * K, 3 * K)) + list(range(0, 2 * K))
GATES_AFTER = [range(0, K), range(K, 2 * K), range(2 * K, G3), range(0)]


def counts(eng, first):
    known = {}

    def at(n):
        if isinstance(first, int):
            return first + n
        if n not in known:
            known[n] = eng.snap(first + n)
        return known[n]
    return at


def build(nc, x, cond, W_ih, W_hh, b_ih, b_hh, coupling, fhn_bias, rms_w, Wk, Wo, ln_g, ln_b, out):
    ctx = ExitStack()
    with ctx:
        def sb(name, shape, dt=fp32):
            return ctx.enter_context(nc.sbuf_tensor(name, shape, dt))

        def ps(name, shape, dt=fp32):
            return ctx.enter_context(nc.psum_tensor(name, shape, dt))

        def sem(name):
            return ctx.enter_context(nc.semaphore(name))

        xT_all = sb("xT", [P, T + UNROLL + 3, K, B])
        xT = xT_all[:, 1:T + 1, :, :]
        space = sb("space", [P, 47 * D])
        XC = UNROLL * B
        xpart = sb("xpart", [P, 2, UNROLL * KB], fp16)
        gisum = sb("gisum", [P, G3, XC])
        gi = sb("gi", [P, G3, UNROLL, B])
        whh = sb("whh", [P, 2, K, 3 * D], fp16)
        cpl = sb("cpl", [P, 2, K, D], fp16)
        wih = sb("wih", [P, K, 3 * D])
        xrow = sb("xrow", [P, 2, K, D])
        ident = sb("ident", [P, P])
        NS = KB + 2 * G3 + K
        condT = sb("condT", [P, K, B])
        bias3 = sb("bias3", [P, 4, G3])
        fbias = sb("fbias", [P, K])
        amax = sb("amax", [P, 4 + B])
        amaxa = sb("amaxa", [P, 4 + B])
        pow2 = sb("pow2", [P, 5])
        scale = sb("scale", [P, 5])
        kapx = sb("kapx", [P, 2])
        sprod = sb("sprod", [P, 1])
        inv = sb("inv", [P, 2])
        kap = sb("kap", [P, 5])
        negc3 = sb("negc3", [P, 1])
        h = sb("h", [P, KB])
        hpart = sb("hpart", [P, K, 2, B], fp16)
        gates = sb("gates", [P, GC])
        rz = sb("rz", [P, 2 * KB])
        gated = sb("gated", [P, KB])
        narg = sb("narg", [P, KB])
        cand = sb("cand", [P, KB])
        hdiff = sb("hdiff", [P, KB])
        zdiff = sb("zdiff", [P, KB])
        q1raw = sb("q1raw", [P, KB])
        q1 = sb("q1", [P, KB])
        tfull = sb("tfull", [P, KB])
        tpart = sb("tpart", [P, 2, K, 2, B], fp16)
        sq = sb("sq", [P, 4, KB])
        sqkept = sb("sqkept", [P, KB])
        cub = sb("cub", [P, KB])
        qhat = sb("qhat", [P, 4, KB])
        phat = sb("phat", [P, KB])
        x1 = sb("x1", [P, KB])
        x1keep = sb("x1keep", [P, KB])
        uscaled = sb("uscaled", [P, KB])
        uhat = sb("uhat", [P, KB])
        drive0 = sb("drive0", [P, KB])
        udrive = sb("udrive", [P, 4, KB])
        psum_p = sb("psum_p", [P, 4, KB])
        sums0 = sb("sums0", [P, 4, KB])
        sums = sb("sums", [P, 4, KB])
        term = sb("term", [P, 4, KB])
        coef = sb("coef", [P, 5, 4, KB])
        konst = sb("konst", [P, 4, KB])
        scol = sb("scol", [P, KB])
        bhat = sb("bhat", [P, KB])
        clampc = sb("clampc", [P, 2])
        ones = sb("ones", [P, KB])

        bank = 512
        psum = ps("psum", [P, 8 * bank])

        def triple(first, stride):
            return psum[:, first:first + 3 * stride].rearrange("p (s c) -> p s c", c=stride)

        half = bank // 2
        stage_base = psum[:, bank:bank + KB]
        stage3 = [triple(0, half), triple(bank + HC, bank - HC)]
        stage_out = [stage3[0][:, 0:2, :], stage3[1][:, 1:3, :]]
        gate_base = psum[:, 4 * bank:4 * bank + GC]
        gate3 = [triple(3 * bank, half), triple(4 * bank + 2 * KB, bank - 2 * KB)]
        gate_out = [gate3[0][:, 0:2, :], gate3[1][:, 1:3, :]]
        qt = psum[:, 6 * bank:8 * bank].rearrange("p (a c) -> p a c", c=bank)[:, :, 0:HC]
        banks = [psum[:, i * bank:(i + 1) * bank] for i in range(8)]
        bounce, pwork, pscore = banks[0:4], banks[5:8], banks[4]
        cbank = pwork + [pscore]
        pgi = psum[:, 4 * bank + 4 * KB:4 * bank + 4 * KB + G3 * 2 * XC]

        wihp = space[:, 0:K * 3 * D].bitcast(fp16).rearrange("p (w k n) -> p w k n", w=2, k=K)
        w_row = space[:, K * 3 * D:2 * K * 3 * D].rearrange("p (k n) -> p k n", k=K)
        c_row = space[:, 24 * D:24 * D + K * D].rearrange("p (n k) -> p n k", n=K)
        small = space[0:NS, 28 * D:28 * D + P]

        wih_flat = wih[:, :, :].rearrange("p k n -> p (k n)")
        wk_row = wih_flat[:, 0:K * D].rearrange("p (n d) -> p n d", n=K)
        wo_row = wih_flat[:, K * D:2 * K * D].rearrange("p (n d) -> p n d", n=K)
        x3T = wih_flat[:, 0:2 * D].rearrange("p (a k t) -> p a k t", a=2, k=K)
        ytile = wih_flat[:, 2 * D:6 * D].rearrange("p (a d) -> p a d", a=4)
        rows = xrow[:, :, :, :].rearrange("p a n d -> p (a n d)")
        grid = rows[:, 0:B * D].rearrange("p (b d) -> p b d", b=B)
        rms_row, gamma_row, beta_row, query_row = [rows[:, (B + i) * D:(B + i + 1) * D] for i in range(4)]

        def take(at, n):
            return space[:, at * D:(at + n) * D]

        spread = take(0, B * K).rearrange("p (b k l) -> p b k l", b=B, k=K)
        normed = take(16, 8).rearrange("p (a n d) -> p a n d", a=2, n=K)
        x3 = take(24, 8).rearrange("p (a n d) -> p a n d", a=2, n=K)
        projb = take(32, 4).rearrange("p (b d) -> p b d", b=B)
        wkT = take(36, 4).rearrange("p (k n) -> p k n", k=K)
        woT = take(40, 4).rearrange("p (k n) -> p k n", k=K)
        scratch = take(44, 1)
        proj4 = take(45, 1)[0:B, :]
        keyq = take(46, 1)
        x2s_a = whh[:, 0, :, :].rearrange("p k n -> p (k n)").bitcast(fp32)[:, 0:K * D].rearrange("p (n d) -> p n d", n=K)
        x2s_b = whh[:, 1, :, :].rearrange("p k n -> p (k n)").bitcast(fp32)[:, 0:K * D].rearrange("p (n d) -> p n d", n=K)
        x2s = [x2s_a, x2s_b]
        NB = B * BLOCKS
        blk = wih_flat[:, 9 * D + P:9 * D + 2 * P].rearrange("p (k b n) -> p k b n", k=K, b=B)
        weighted = wih_flat[:, 8 * D:8 * D + K * NB].rearrange("p (k b n) -> p k b n", k=K, b=B)
        att = sb("att", [P, K, B])
        feature = sb("feature", [P, K])
        sumsq = sb("sumsq", [NB, 1])
        dot = sb("dot", [NB, 1])
        root = sb("root", [P, 4])
        newton = sb("newton", [P, 3, 4])
        score = sb("score", [NB, 1])
        srow = sb("srow", [1, 5, B, BLOCKS])
        smax = sb("smax", [1, 3, B])
        onerow = wih_flat[0:1, 9 * D:9 * D + P]
        pick = wih_flat[0:B, 10 * D:11 * D].rearrange("p (b m) -> p b m", b=B)
        stats = sb("stats", [P, K, 6])
        moments = sb("moments", [P, 2, K, 2])
        shift = sb("shift", [P, 2, K])
        rstd = sb("rstd", [P, 2, K])

        hn_base_ready = sem("hn_base_ready")
        small_turned = sem("small_turned")
        in_small, in_wih, in_whh, in_c = sem("in_small"), sem("in_wih"), sem("in_whh"), sem("in_c")
        in_x = [sem(f"in_x{i}") for i in range(2)]
        ident_ready, ident_raw = sem("ident_ready"), sem("ident_raw")
        amax_ready, amax_all, linked = sem("amax_ready"), sem("amax_all"), sem("linked")
        consts_ready = sem("consts_ready")
        turned = sem("turned")
        cturned = sem("cturned")
        gi_mm, gi_summed = [[sem(f"{name}_{part}") for part in ("rz", "n")] for name in ("gi_mm", "gi_summed")]
        gi_ready = sem("gi_ready")
        x_hi, x_parts = sem("x_hi"), sem("x_parts")
        scales_ready, w_hi, wih_ready = sem("scales_ready"), sem("w_hi"), sem("wih_ready")
        whh_ready = sem("whh_ready")
        xT_ready, cpl_ready, tanh0_ready = sem("xT_ready"), sem("cpl_ready"), sem("tanh0_ready")

        h_parts, gibase_ready = sem("h_parts"), sem("gibase_ready")
        nr_mm, z_mm, nr_sum, z_sum = sem("nr_mm"), sem("z_mm"), sem("nr_sum"), sem("z_sum")
        r_ready, z_ready, gated_ready, narg_ready = sem("r_ready"), sem("z_ready"), sem("gated_ready"), sem("narg_ready")
        cand_ready, hdiff_ready, zdiff_ready = sem("cand_ready"), sem("hdiff_ready"), sem("zdiff_ready")
        h_ready, h_hi = sem("h_ready"), sem("h_hi")

        t_parts = [[sem(f"t_parts{s}{a}") for a in "ab"] for s in range(4)]
        stage_mm = [[sem(f"stage_mm{s}{a}") for a in "ab"] for s in range(4)]
        stage_sum = [[sem(f"stage_sum{s}{a}") for a in "ab"] for s in range(4)]
        tanh_ready = [[sem(f"tanh_ready{s}{a}") for a in "ab"] for s in range(4)]
        sq_ready = [sem(f"sq_ready{s}") for s in range(4)]
        qhat_ready = [sem(f"qhat_ready{s}") for s in range(4)]
        cub_ready = [sem(f"cub_ready{s}") for s in range(4)]
        base_ready = [sem(f"base_ready{s}") for s in range(4)]
        term_ready = [sem(f"term_ready{s}") for s in range(4)]
        sums_ready = [sem(f"sums_ready{s}") for s in range(4)]
        q1raw_ready, q1_ready, sqkept_ready = sem("q1raw_ready"), sem("q1_ready"), sem("sqkept_ready")
        x1_ready, uscaled_ready, uhat_ready = sem("x1_ready"), sem("uscaled_ready"), sem("uhat_ready")
        phat_ready, psum_p_ready, sums0_ready = sem("phat_ready"), sem("psum_p_ready"), sem("sums0_ready")
        drive0_ready, x2_ready, x1keep_ready = sem("drive0_ready"), sem("x2_ready"), sem("x1keep_ready")
        out_sem = [sem(f"out_sem{i}") for i in range(2 * K)]
        in_mats, in_rows = sem("in_mats"), sem("in_rows")
        pick_ready = sem("pick_ready")
        dist_ready, spread_ready = sem("dist_ready"), sem("spread_ready")
        mats_turned, mats_ready = sem("mats_turned"), sem("mats_ready")
        blk_ready, keys_mm, sumsq_ready = sem("blk_ready"), sem("keys_mm"), sem("sumsq_ready")
        score_ready, srow_mm, sexp_in, sexp_ready = sem("score_ready"), sem("srow_mm"), sem("sexp_in"), sem("sexp_ready")
        attn_ready, attn_mm, att_ready = sem("attn_ready"), sem("attn_mm"), sem("att_ready")
        proj_mm, proj4_ready, projb_mm, projb_ready = sem("proj_mm"), sem("proj4_ready"), sem("projb_mm"), sem("projb_ready")
        var_ready, root_ready = sem("var_ready"), sem("root_ready")
        x2_turned, x2s_ready, y_ready, stats_ready = sem("x2_turned"), sem("x2s_ready"), sem("y_ready"), sem("stats_ready")
        rstd_ready = sem("rstd_ready")
        normed_ready, scaled_ready, shifted_ready, x3_ready = sem("normed_ready"), sem("scaled_ready"), sem("shifted_ready"), sem("x3_ready")
        x3_turned, x3T_ready, sample_mm, final_ready = sem("x3_turned"), sem("x3T_ready"), sem("sample_mm"), sem("final_ready")

        block = ctx.enter_context(nc.Block())

        @block.sync
        def _(sp):
            def load_x(b):
                sp.dma_start(xrow[:, b % 2, :, :], x[b].rearrange("(n p) d -> p n d", p=P)).then_inc(in_x[b % 2], 16)

            sp.dma_start(w_row, W_hh.rearrange("(k p) n -> p k n", p=P)).then_inc(in_whh, 16)
            sp.dma_start(c_row, coupling.rearrange("(n p) k -> p n k", p=P)).then_inc(in_c, 16)
            sp.dma_start(wih[:, :, :], W_ih.rearrange("(k p) n -> p k n", p=P)).then_inc(in_wih, 16)
            load_x(0)
            load_x(1)
            for b in range(2, B):
                sp.wait_ge(turned, K * (b - 1))
                load_x(b)
            sp.wait_ge(turned, B * K)
            sp.dma_start(grid.rearrange("p b d -> p (b d)"),
                         cond.rearrange("b d -> (b d)").unsqueeze(0).broadcast_to([P, B * D])).then_inc(in_rows, 16)
            for dst, src in ((rms_row, rms_w), (gamma_row, ln_g), (beta_row, ln_b), (query_row, cond[1])):
                sp.dma_start(dst, src.unsqueeze(0).broadcast_to([P, D])).then_inc(in_rows, 16)
            sp.wait_ge(wih_ready, 1)
            sp.dma_start(wk_row, Wk.rearrange("(n p) d -> p n d", p=P)).then_inc(in_mats, 16)
            sp.dma_start(wo_row, Wo.rearrange("(n p) d -> p n d", p=P)).then_inc(in_mats, 16)
            for e in range(B * K):
                sp.wait_ge(final_ready, e + 1)
                sp.dma_start(out[e // K, (e % K) * P:(e % K + 1) * P, :], normed[:, e // K % 2, e % K, :]).then_inc(out_sem[e % (2 * K)], 16)
            for place in range(2 * K):
                sp.wait_ge(out_sem[place], 16 * (B // 2))

        @block.gpsimd
        def _(pool):
            pool.memset(ident[:, :], 0.0).then_inc(ident_raw, 1)
            pool.wait_ge(ident_raw, 1)
            pool.affine_select(out=ident[:, :], in_=ident[:, :], compare_op=ALU.not_equal, fill=1.0, base=0,
                               pattern=[[-1, P]], channel_multiplier=1).then_inc(ident_ready, 1)
            sums_of = recovery_sums()
            for src in range(5):
                for r in range(4):
                    pool.memset(coef[:, src, r, :], sums_of[r][src])
            pool.iota(feature[:, :], pattern=[[-P, K]], base=0, channel_multiplier=-1,
                      allow_small_or_imprecise_dtypes=True)
            pool.memset(ones[:, :], 1.0)
            pool.memset(xT_all[:, T + 1:T + UNROLL + 3, :, :], 0.0)
            pool.memset(x1keep[:, :], 0.0)
            pool.wait_ge(amax_ready, 4)
            pool.partition_all_reduce(amaxa[:, 0:4], amax[:, 0:4], P, bass.bass_isa.ReduceOp.max).then_inc(amax_all, 1)
            pool.wait_ge(amax_ready, 4 + B)
            pool.partition_all_reduce(amaxa[:, 4:4 + B], amax[:, 4:4 + B], P, bass.bass_isa.ReduceOp.max).then_inc(amax_all, 1)
            pool.wait_ge(phat_ready, 1)

            def next_drive(v, t_next):
                pool.wait_ge(h_ready, v)
                pool.tensor_tensor(x1[:, :], xT_all[:, t_next + 1, :, :].rearrange("p k b -> p (k b)"), h[:, :],
                                   ALU.add).then_inc(x1_ready, 1)
                pool.wait_ge(x1_ready, v)
                pool.tensor_tensor(uscaled[:, :], x1[:, :], scol[:, :], ALU.mult).then_inc(uscaled_ready, 1)
                pool.wait_ge(uscaled_ready, v)
                pool.tensor_tensor(uhat[:, :], uscaled[:, :], bhat[:, :], ALU.add).then_inc(uhat_ready, 1)
                pool.wait_ge(uhat_ready, v)
                pool.tensor_tensor(udrive[:, 0:3, :], konst[:, 0:3, :],
                                   uhat[:, :].unsqueeze(1).broadcast_to([P, 3, KB]), ALU.add)

            def start_sums(v):
                pool.wait_ge(phat_ready, v)
                pool.tensor_tensor(drive0[:, :], uhat[:, :], phat[:, :], ALU.subtract).then_inc(drive0_ready, 1)
                pool.tensor_tensor(psum_p[:, :, :], coef[:, 0, :, :],
                                   phat[:, :].unsqueeze(1).broadcast_to([P, 4, KB]), ALU.mult).then_inc(psum_p_ready, 1)
                pool.wait_ge(psum_p_ready, v)
                pool.tensor_tensor(sums0[:, :, :], psum_p[:, :, :], udrive[:, :, :], ALU.add).then_inc(sums0_ready, 1)

            pool.wait_ge(whh_ready, 1)
            pool.wait_ge(cpl_ready, 1)
            next_drive(1, 0)
            start_sums(1)

            def step(at, u):
                now, tail = at(u + 1), at(u + 2)
                pool.wait_ge(q1_ready, now)
                pool.tensor_tensor(qhat[:, 0, :], q1[:, :], scol[:, :], ALU.mult).then_inc(qhat_ready[0], 1)
                pool.wait_ge(qhat_ready[0], now)
                pool.tensor_tensor(term[:, :, :], coef[:, 1, :, :],
                                   qhat[:, 0, :].unsqueeze(1).broadcast_to([P, 4, KB]), ALU.mult).then_inc(term_ready[0], 1)
                pool.wait_ge(sums0_ready, now)
                pool.wait_ge(term_ready[0], now)
                pool.tensor_tensor(sums[:, :, :], sums0[:, :, :], term[:, :, :], ALU.add).then_inc(sums_ready[0], 1)
                for s, lo in ((1, 1), (2, 2), (3, 2)):
                    pool.wait_ge(qhat_ready[s], now)
                    pool.wait_ge(sums_ready[s - 1], now)
                    pool.tensor_tensor(term[:, lo:4, :], coef[:, 1 + s, lo:4, :],
                                       qhat[:, s, :].unsqueeze(1).broadcast_to([P, 4 - lo, KB]),
                                       ALU.mult).then_inc(term_ready[s], 1)
                    pool.wait_ge(term_ready[s], now)
                    pool.tensor_tensor(sums[:, lo:4, :], sums[:, lo:4, :], term[:, lo:4, :],
                                       ALU.add).then_inc(sums_ready[s], 1)
                    if s == 1:
                        pool.wait_ge(x2_ready, now)
                        pool.tensor_tensor(x1keep[:, :], x1[:, :], ones[:, :], ALU.mult).then_inc(x1keep_ready, 1)
                        pool.wait_ge(x1keep_ready, now)
                        next_drive(tail, now)
                start_sums(tail)

            with pool.Fori(0, T - UNROLL + 1, UNROLL) as t:
                at = counts(pool, t)
                for u in range(UNROLL):
                    step(at, u)

            pool.wait_ge(wih_ready, 1)
            pool.memset(onerow[:, :], 1.0)
            pool.memset(pick[:, :, :], 0.0).then_inc(pick_ready, 1)
            pool.wait_ge(pick_ready, 1)
            pool.affine_select(out=pick[:, :, :], in_=pick[:, :, :], compare_op=ALU.not_equal, fill=1.0, base=0,
                               pattern=[[-1, B], [0, P]], channel_multiplier=1).then_inc(pick_ready, 1)
            for b in range(B):
                for n in range(K):
                    e = b * K + n
                    pool.wait_ge(y_ready, e + 1)
                    pool.tensor_tensor(x2s[b % 2][:, n, :], x2s[b % 2][:, n, :], beta_row, ALU.add).then_inc(shifted_ready, 1)

        @block.scalar
        def _(act):
            for src, at, n in ((cond.rearrange("b (k p) -> (b k) p", p=P), 0, KB),
                               (b_ih.rearrange("(n p) -> n p", p=P), KB, G3),
                               (b_hh.rearrange("(n p) -> n p", p=P), KB + G3, G3),
                               (fhn_bias.rearrange("(n p) -> n p", p=P), KB + 2 * G3, K)):
                act.dma_start(small[at:at + n, :], src).then_inc(in_small, 16)
            def turn_x(b):
                for n in range(K):
                    e = b * K + n
                    act.wait_ge(turned, e + 1)
                    act.activation(xT[:, n * P:(n + 1) * P, :, b].rearrange("p t k -> p k t"),
                                   bounce[e % 4].rearrange("p (k t) -> p k t", k=K), ACT.Copy).then_inc(xT_ready, 1)

            turn_x(0)
            turn_x(1)
            act.wait_ge(scales_ready, 1)
            for k in range(K):
                act.activation(whh[:, 0, k, :], w_row[:, k, :], ACT.Identity, scale=scale[:, 0:1]).then_inc(w_hi, 1)
            for k in range(K):
                act.activation(wihp[:, 0, k, :], wih[:, k, :], ACT.Identity, scale=scale[:, 3:4]).then_inc(w_hi, 1)
            turn_x(2)
            turn_x(3)
            act.wait_ge(hn_base_ready, 1)
            k_gate, k_prod, k_half, k_full, k_sixth = [act.alloc_register(f"act_scale{i}") for i in range(5)]
            for n, r in enumerate((k_gate, k_prod, k_half, k_full, k_sixth)):
                act.reg_load(r, kap[0:1, n:n + 1].bitcast(i32))
            k_h = act.alloc_register("act_scale_h")
            act.reg_load(k_h, scale[0:1, 2:3].bitcast(i32))
            k_stage = [k_half, k_half, k_full, k_sixth]

            def gate_input(v, u, read, group=None):
                if read is not None:
                    act.wait_ge(z_sum, read)
                if group is not None:
                    act.wait_ge(gi_ready, group)
                act.activation(gate_base[:, KB:3 * KB].rearrange("p (n b) -> p n b", b=B),
                               gi[:, 0:2 * K, u, :], ACT.Copy,
                               scale=k_prod).then_inc(gibase_ready, 1)

            def sigmoid_r(v):
                act.wait_ge(nr_sum, v)
                act.activation(rz[:, 0:KB], gates[:, KB:2 * KB], ACT.Sigmoid, scale=k_gate).then_inc(r_ready, 1)

            def sigmoid_z(v):
                act.wait_ge(z_sum, v)
                act.activation(rz[:, KB:2 * KB], gates[:, 2 * KB:3 * KB], ACT.Sigmoid, scale=k_gate).then_inc(z_ready, 1)

            def candidate(v):
                act.wait_ge(narg_ready, v)
                act.activation(cand[:, :], narg[:, :], ACT.Tanh).then_inc(cand_ready, 1)

            def h_high(v, made):
                act.wait_ge(h_ready, made)
                act.activation(hpart[:, :, 0, :], h[:, :].rearrange("p (k b) -> p k b", b=B), ACT.Copy,
                               scale=k_h).then_inc(h_hi, 1)

            for v in (1, 2):
                gate_input(v, v - 1, v - 1 if v > 1 else None, group=UNROLL)
                sigmoid_r(v)
                candidate(v)
                sigmoid_z(v)
            first = condT[:, :, :].rearrange("p k b -> p (k b)")
            for a in range(HALVES):
                act.activation(tpart[:, 0, a * HK:(a + 1) * HK, 0, :], condT[:, a * HK:(a + 1) * HK, :], ACT.Tanh)
                act.activation(tfull[:, a * HC:(a + 1) * HC], first[:, a * HC:(a + 1) * HC], ACT.Tanh).then_inc(tanh0_ready, 1)

            def step(at, u):
                now, tail, gru = at(u + 1), at(u + 2), at(u + 3)
                for s in range(4):
                    for a in range(HALVES):
                        act.wait_ge(stage_sum[s][a], now)
                        act.activation(tpart[:, (s + 1) % 2, a * HK:(a + 1) * HK, 0, :], qt[:, a, :].rearrange("p (k b) -> p k b", b=B),
                                       ACT.Tanh, scale=k_stage[s])
                        act.activation(tfull[:, a * HC:(a + 1) * HC], qt[:, a, :], ACT.Tanh,
                                       scale=k_stage[s]).then_inc(tanh_ready[s][a], 1)
                    if s < 3:
                        act.activation(sq[:, s + 1, :].rearrange("p (a c) -> p a c", a=HALVES), qt, ACT.Square,
                                       scale=k_stage[s]).then_inc(sq_ready[s + 1], 1)
                        act.activation(qhat[:, s + 1, :].rearrange("p (a c) -> p a c", a=HALVES), qt, ACT.Copy,
                                       scale=STEP[s]).then_inc(qhat_ready[s + 1], 1)
                    else:
                        act.activation(q1raw[:, :].rearrange("p (a c) -> p a c", a=HALVES), qt, ACT.Copy,
                                       scale=k_stage[s]).then_inc(q1raw_ready, 1)
                        act.activation(sq[:, 0, :].rearrange("p (a c) -> p a c", a=HALVES), qt, ACT.Square,
                                       scale=k_stage[s]).then_inc(sq_ready[0], 1)
                        h_high(at(u + 4), gru)
                    if s == 1:
                        gate_input(gru, u, tail, group=at(2 * UNROLL) if u == 0 else None)
                        sigmoid_r(gru)
                    if s == 2:
                        candidate(gru)
                        sigmoid_z(gru)

            with act.Fori(0, T - UNROLL + 1, UNROLL) as t:
                at = counts(act, t)
                for u in range(UNROLL):
                    step(at, u)

            for k in range(2 * K):
                act.wait_ge(mats_turned, k + 1)
                act.activation(wkT[:, k, :] if k < K else woT[:, k - K, :], bounce[k % 4], ACT.Copy).then_inc(mats_ready, 1)
            def row_out(b, n):
                e = b * K + n
                act.wait_ge(x2_turned, e + 1)
                if b >= 2:
                    act.wait_ge(x3_ready, e - 2 * K + 1)
                act.activation(x2s[b % 2][:, n, :], bounce[e % 2], ACT.Copy).then_inc(x2s_ready, 1)

            for b in range(2):
                for n in range(K):
                    row_out(b, n)

            def distances(b):
                for k in range(K):
                    act.activation(spread[:, b, k, :], grid[:, b, :], ACT.Abs, bias=feature[:, k:k + 1]).then_inc(dist_ready, 1)

            distances(0)
            act.wait_ge(keys_mm, 1)
            act.activation(scratch[0:NB, :], pwork[0][0:NB, :], ACT.Square, accum_out=sumsq[:, :]).then_inc(sumsq_ready, 1)
            act.wait_ge(var_ready, 1)
            act.activation(root[0:NB, 0:1], newton[0:NB, 0, 0:1], ACT.Sqrt).then_inc(root_ready, 1)
            act.wait_ge(sexp_in, 1)
            act.activation(srow[:, 2, :, :], srow[:, 1, :, :], ACT.Exp).then_inc(sexp_ready, 1)
            act.wait_ge(proj_mm, 1)
            act.activation(proj4, pwork[2][0:B, :], ACT.Copy).then_inc(proj4_ready, 1)
            for b in range(B):
                act.wait_ge(projb_mm, b + 1)
                act.activation(projb[:, b, :], bounce[b], ACT.Copy).then_inc(projb_ready, 1)

            def deviation(b):
                act.wait_ge(var_ready, b + 2)
                act.activation(root[:, :], newton[:, 0, :], ACT.Sqrt).then_inc(root_ready, 1)

            def normalize(b, n):
                e = b * K + n
                act.wait_ge(rstd_ready, b + 1)
                if b >= 2:
                    act.wait_ge(out_sem[e % (2 * K)], 16)
                act.activation(normed[:, b % 2, n, :], ytile[:, n, :], ACT.Identity, bias=shift[:, b % 2, n:n + 1],
                               scale=rstd[:, b % 2, n:n + 1]).then_inc(normed_ready, 1)

            deviation(0)
            for n in range(K):
                normalize(0, n)
            distances(1)
            for b in range(B):
                for n in range(K):
                    e = b * K + n
                    act.wait_ge(x3_turned, e + 1)
                    if e >= 2:
                        act.wait_ge(sample_mm, e - 1)
                    act.activation(x3T[:, e % 2, :, :].rearrange("p k t -> p (k t)"), bounce[2 + e % 2], ACT.Copy).then_inc(x3T_ready, 1)
                    if b == 0 and n == 1:
                        deviation(1)
                        normalize(1, 0)
                        normalize(1, 1)
                    elif b + 1 < B and (b > 0 or n > 1):
                        normalize(b + 1, n)
                    if b + 2 < B:
                        row_out(b + 2, n)
                if b + 2 < B:
                    deviation(b + 2)
                    distances(b + 2)

        @block.vector
        def _(dve):
            done = [0]

            def link(ins):
                done[0] += 1
                ins.then_inc(linked, 1)
                dve.wait_ge(linked, done[0])

            dve.wait_ge(small_turned, 1)
            link(dve.tensor_copy(condT[:, :, :].rearrange("p k b -> p b k"),
                                 pwork[0][:, 0:KB].rearrange("p (b k) -> p b k", k=K)))
            link(dve.tensor_copy(bias3[:, 0:2, :].rearrange("p a n -> p (a n)"), pwork[0][:, KB:KB + 2 * G3]))
            link(dve.tensor_copy(fbias[:, :], pwork[0][:, KB + 2 * G3:NS]))
            link(dve.tensor_copy(bias3[:, 2, :], bias3[:, 0, :]))
            dve.tensor_tensor(bias3[:, 2, 0:2 * K], bias3[:, 0, 0:2 * K], bias3[:, 1, 0:2 * K],
                              ALU.add).then_inc(consts_ready, 1)
            dve.tensor_reduce(amax[:, 2:3], condT[:, :, :].rearrange("p k b -> p (k b)"), AX.X, ALU.max,
                              apply_absolute_value=True).then_inc(amax_ready, 1)
            dve.wait_ge(in_whh, 16)
            dve.tensor_reduce(amax[:, 0:1], w_row, AX.XY, ALU.max, apply_absolute_value=True).then_inc(amax_ready, 1)
            dve.wait_ge(in_c, 16)
            dve.tensor_reduce(amax[:, 1:2], c_row, AX.XY, ALU.max, apply_absolute_value=True).then_inc(amax_ready, 1)
            dve.wait_ge(in_wih, 16)
            dve.tensor_reduce(amax[:, 3:4], wih[:, :, :], AX.XY, ALU.max, apply_absolute_value=True).then_inc(amax_ready, 1)
            dve.wait_ge(amax_all, 1)
            link(dve.tensor_scalar(amaxa[:, 2:3], amaxa[:, 2:3], 1.0, None, ALU.max))

            def powers(lo, hi):
                link(dve.tensor_scalar(amaxa[:, lo:hi], amaxa[:, lo:hi], 2.0 ** -40, None, ALU.max))
                link(dve.tensor_scalar(pow2[:, lo:hi].bitcast(i32), amaxa[:, lo:hi].bitcast(i32), 0x7F800000, None, ALU.bitwise_and))
                link(dve.reciprocal(scale[:, lo:hi], pow2[:, lo:hi]))
                dve.tensor_scalar(scale[:, lo:hi], scale[:, lo:hi], 2.0 ** 14, None, ALU.mult).then_inc(scales_ready, 1)

            powers(0, 4)
            dve.wait_ge(scales_ready, 1)
            s_i, s_x = scale[:, 3:4], scale[:, 4:5]
            s_w, s_c, s_h = scale[:, 0:1], scale[:, 1:2], scale[:, 2:3]
            link(dve.tensor_tensor(kap[:, 1:2], s_w, s_h, ALU.mult))
            link(dve.reciprocal(kap[:, 0:1], kap[:, 1:2]))
            link(dve.reciprocal(inv[:, 1:2], s_c))
            for n, c in ((2, DT / 2), (3, DT), (4, DT / 6)):
                link(dve.tensor_scalar(kap[:, n:n + 1], inv[:, 1:2], c, None, ALU.mult))
            link(dve.tensor_scalar(negc3[:, :], s_c, -1.0 / 3.0, None, ALU.mult))
            link(dve.tensor_scalar(clampc[:, 0:1], s_c, CLAMP, None, ALU.mult))
            link(dve.tensor_scalar(clampc[:, 1:2], s_c, -CLAMP, None, ALU.mult))
            link(dve.memset(konst[:, :, :], 1.0))
            sums_of = recovery_sums()
            for r in range(4):
                link(dve.tensor_scalar(konst[:, r, :], konst[:, r, :], sums_of[r][5], s_c, ALU.mult, ALU.mult))
            link(dve.tensor_copy(udrive[:, 3, :], konst[:, 3, :]))
            link(dve.memset(scol[:, :], 1.0))
            link(dve.tensor_scalar(scol[:, :], scol[:, :], s_c, None, ALU.mult))
            link(dve.tensor_tensor(bhat[:, :].rearrange("p (k b) -> p k b", b=B),
                                   scol[:, :].rearrange("p (k b) -> p k b", b=B),
                                   fbias[:, :].unsqueeze(2).broadcast_to([P, K, B]), ALU.mult))
            link(dve.tensor_scalar(bias3[:, 3, :], bias3[:, 1, :], kap[:, 1:2], None, ALU.mult))
            cT = condT[:, :, :].rearrange("p k b -> p (k b)")
            dve.tensor_copy(q1[:, :], cT).then_inc(q1_ready, 1)
            link(dve.tensor_copy(h[:, :], cT))
            dve.tensor_scalar(phat[:, :], cT, s_c, None, ALU.mult).then_inc(phat_ready, 1)
            for k in range(K):
                dve.wait_ge(w_hi, k + 1)
                ins = dve.scalar_tensor_tensor(whh[:, 1, k, :], w_row[:, k, :], s_w, whh[:, 0, k, :],
                                               ALU.mult, ALU.subtract)
            ins.then_inc(whh_ready, 1)
            for k in range(K):
                dve.wait_ge(w_hi, K + k + 1)
                ins = dve.scalar_tensor_tensor(wihp[:, 1, k, :], wih[:, k, :], s_i, wihp[:, 0, k, :],
                                               ALU.mult, ALU.subtract)
            ins.then_inc(wih_ready, 1)
            for k in range(K):
                dve.wait_ge(cturned, k + 1)
                link(dve.tensor_scalar(cpl[:, 0, k, :], cbank[k], s_c, None, ALU.mult))
                ins = dve.scalar_tensor_tensor(cpl[:, 1, k, :], cbank[k], s_c, cpl[:, 0, k, :],
                                               ALU.mult, ALU.subtract)
            ins.then_inc(cpl_ready, 1)
            for b in range(B):
                dve.wait_ge(xT_ready, K * (b + 1))
                dve.tensor_reduce(amax[:, 4 + b:5 + b], xT[:, :, :, b], AX.XY, ALU.max,
                                  apply_absolute_value=True).then_inc(amax_ready, 1)
            dve.wait_ge(amax_all, 2)
            link(dve.tensor_reduce(amaxa[:, 4:5], amaxa[:, 4:4 + B], AX.X, ALU.max))
            powers(4, 5)
            dve.wait_ge(scales_ready, 2)
            link(dve.tensor_tensor(kapx[:, 0:1], s_i, s_x, ALU.mult))
            link(dve.reciprocal(kapx[:, 1:2], kapx[:, 0:1]))

            def split_x_high(slot, v):
                steps = xT_all[:, bass.ds(slot, UNROLL), :, :].rearrange("p t k b -> p (t k b)")
                dve.tensor_scalar(xpart[:, 0, :], steps, s_x, None, ALU.mult).then_inc(x_hi, UNROLL)

            def split_x_low(slot, v):
                steps = xT_all[:, bass.ds(slot, UNROLL), :, :].rearrange("p t k b -> p (t k b)")
                dve.wait_ge(x_hi, v)
                dve.scalar_tensor_tensor(xpart[:, 1, :], steps, s_x, xpart[:, 0, :],
                                         ALU.mult, ALU.subtract).then_inc(x_parts, UNROLL)

            RZ, N = 0, 1
            tiles_of = [slice(0, 2 * K), slice(2 * K, G3)]

            def sum_inputs(part, v):
                dve.wait_ge(gi_mm[part], v)
                dve.tensor_reduce(gisum[:, tiles_of[part], :],
                                  pgi.rearrange("p (n a c) -> p n c a", n=G3, a=2)[:, tiles_of[part], :, :],
                                  AX.X, ALU.add).then_inc(gi_summed[part], UNROLL)

            def bias_inputs(part, v):
                tiles = tiles_of[part]
                dve.wait_ge(gi_summed[part], v)
                ins = dve.scalar_tensor_tensor(gi[:, tiles, :, :].rearrange("p n t b -> p n (t b)"), gisum[:, tiles, :],
                                         kapx[:, 1:2],
                                         bias3[:, 2, tiles].unsqueeze(2).broadcast_to([P, tiles.stop - tiles.start, XC]),
                                         ALU.mult, ALU.add)
                if part == RZ:
                    ins.then_inc(gi_ready, UNROLL)

            split_x_high(1, UNROLL)
            split_x_low(1, UNROLL)
            dve.wait_ge(gi_mm[N], UNROLL)
            for part in (RZ, N):
                sum_inputs(part, UNROLL)
                bias_inputs(part, UNROLL)
            dve.tensor_copy(gate_base[:, 0:KB].rearrange("p (k b) -> p k b", b=B),
                            bias3[:, 3, 2 * K:3 * K].unsqueeze(2).broadcast_to([P, K, B])).then_inc(hn_base_ready, 1)
            dve.wait_ge(hn_base_ready, 1)
            split_x_high(3, 2 * UNROLL)
            split_x_low(3, 2 * UNROLL)

            h3 = h[:, :].rearrange("p (k b) -> p k b", b=B)

            def h_high(v):
                dve.tensor_scalar(hpart[:, :, 0, :], h3, s_h, None, ALU.mult).then_inc(h_hi, 1)

            def h_low(v):
                dve.wait_ge(h_hi, v)
                dve.scalar_tensor_tensor(hpart[:, :, 1, :], h3, s_h, hpart[:, :, 0, :],
                                         ALU.mult, ALU.subtract).then_inc(h_parts, 1)

            def sum_nr(v):
                dve.wait_ge(gibase_ready, v)
                dve.wait_ge(nr_mm, v)
                dve.tensor_reduce(gates[:, 0:2 * KB], gate3[0].rearrange("p s c -> p c s")[:, 0:2 * KB, :],
                                  AX.X, ALU.add).then_inc(nr_sum, 1)

            def sum_z(v):
                dve.wait_ge(z_mm, v)
                dve.tensor_reduce(gates[:, 2 * KB:3 * KB], gate3[1].rearrange("p s c -> p c s")[:, 0:KB, :],
                                  AX.X, ALU.add).then_inc(z_sum, 1)

            def reset(v):
                dve.wait_ge(r_ready, v)
                dve.tensor_tensor(gated[:, :], gates[:, 0:KB], rz[:, 0:KB], ALU.mult).then_inc(gated_ready, 1)

            def argument(v, u):
                dve.wait_ge(gated_ready, v)
                dve.scalar_tensor_tensor(narg[:, :].rearrange("p (k b) -> p k b", b=B),
                                         gated[:, :].rearrange("p (k b) -> p k b", b=B), kap[:, 0:1],
                                         gi[:, 2 * K:3 * K, u, :],
                                         ALU.mult, ALU.add).then_inc(narg_ready, 1)

            def difference(v):
                dve.wait_ge(cand_ready, v)
                dve.tensor_tensor(hdiff[:, :], h[:, :], cand[:, :], ALU.subtract).then_inc(hdiff_ready, 1)

            def weigh(v):
                dve.wait_ge(hdiff_ready, v)
                dve.wait_ge(z_ready, v)
                dve.tensor_tensor(zdiff[:, :], rz[:, KB:2 * KB], hdiff[:, :], ALU.mult).then_inc(zdiff_ready, 1)

            def new_h(v, read=None):
                if read is not None:
                    dve.wait_ge(x1_ready, read)
                dve.wait_ge(zdiff_ready, v)
                dve.tensor_tensor(h[:, :], zdiff[:, :], cand[:, :], ALU.add).then_inc(h_ready, 1)

            dve.wait_ge(in_rows, 80)
            for c1, c2, o1, o2 in ((1.0, 0.5, ALU.add, ALU.mult), (D - 1.0, 0.0, ALU.mult, ALU.max), (D - 1.0, None, ALU.min, None)):
                ins = (dve.tensor_scalar(grid, grid, c1, c2, o1, o2) if o2 else dve.tensor_scalar(grid, grid, c1, None, o1))
                link(ins)
            for v in (1, 2):
                h_high(v)
                h_low(v)
                sum_nr(v)
                reset(v)
                argument(v, v - 1)
                difference(v)
                sum_z(v)
                weigh(v)
                new_h(v, v - 1 if v > 1 else None)
                dve.wait_ge(h_ready, v)
            dve.tensor_tensor(sq[:, 0, :], q1[:, :], q1[:, :], ALU.mult).then_inc(sq_ready[0], 1)
            h_high(3)
            h_low(3)

            def split_tanh(s, a, v, ready, n):
                dve.wait_ge(ready, n)
                dve.scalar_tensor_tensor(tpart[:, s % 2, a * HK:(a + 1) * HK, 1, :],
                                         tfull[:, a * HC:(a + 1) * HC].rearrange("p (k b) -> p k b", b=B), 1.0,
                                         tpart[:, s % 2, a * HK:(a + 1) * HK, 0, :], ALU.mult, ALU.subtract).then_inc(t_parts[s][a], 1)

            for a in range(HALVES):
                split_tanh(0, a, 1, tanh0_ready, a + 1)
            dve.wait_ge(gi_mm[N], 2 * UNROLL)
            sum_inputs(RZ, 2 * UNROLL)
            bias_inputs(RZ, 2 * UNROLL)

            def window(at, u, s, first=False):
                now, tail, gru = at(u + 1), at(u + 2), at(u + 3)
                if s == 0:
                    if not first:
                        dve.wait_ge(q1raw_ready, at(u))
                        dve.tensor_scalar(q1[:, :], q1raw[:, :], CLAMP, -CLAMP, ALU.min, ALU.max).then_inc(q1_ready, 1)
                    dve.wait_ge(sq_ready[0], now)
                    dve.tensor_scalar(sqkept[:, :], sq[:, 0, :], CLAMP * CLAMP, -3.0 * (1 + 1 / STEP[0]),
                                      ALU.min, ALU.add).then_inc(sqkept_ready, 1)
                    if not first:
                        h_low(gru)
                    dve.wait_ge(drive0_ready, now)
                    dve.wait_ge(sqkept_ready, now)
                    dve.tensor_tensor(cub[:, :], sqkept[:, :], q1[:, :], ALU.mult).then_inc(cub_ready[0], 1)
                    dve.wait_ge(cub_ready[0], now)
                    dve.scalar_tensor_tensor(stage_base, cub[:, :], negc3[:, :], drive0[:, :],
                                             ALU.mult, ALU.add).then_inc(base_ready[0], 1)
                else:
                    dve.wait_ge(qhat_ready[s], now)
                    dve.scalar_tensor_tensor(cub[:, :].rearrange("p (a c) -> p a c", a=HALVES),
                                             sq[:, s, :].rearrange("p (a c) -> p a c", a=HALVES), -3.0, qt,
                                             ALU.add, ALU.mult).then_inc(cub_ready[s], 1)
                    if s == 3:
                        difference(gru)
                    if u == 0 and s == 1:
                        sum_inputs(N, at(2 * UNROLL))
                    if u == UNROLL - 1 and s == 1:
                        sum_inputs(RZ, at(3 * UNROLL))
                    dve.wait_ge(sums_ready[s if s == 3 else s - 1], now)
                    dve.wait_ge(cub_ready[s], now)
                    dve.scalar_tensor_tensor(stage_base, cub[:, :], -STEP[s - 1] / 3, sums[:, s - 1, :],
                                             ALU.mult, ALU.add).then_inc(base_ready[s], 1)
                    if u == 0 and s == 2:
                        split_x_high(at(UNROLL + 3), at(3 * UNROLL))
                    if s == 2:
                        sum_nr(gru)
                    if s == 3:
                        sum_z(gru)
                dve.wait_ge(base_ready[s], now)
                for a in range(HALVES):
                    dve.wait_ge(stage_mm[s][a], now)
                    dve.tensor_reduce(qt[:, a, :], stage3[a].rearrange("p s c -> p c s")[:, 0:HC, :],
                                      AX.X, ALU.add).then_inc(stage_sum[s][a], 1)
                    if s == 3 and a == 0:
                        dve.tensor_scalar(phat[:, :], sums[:, 3, :], clampc[:, 0:1], clampc[:, 1:2],
                                          ALU.min, ALU.max).then_inc(phat_ready, 1)
                if s == 0:
                    dve.tensor_tensor(xT_all[:, at(u), :, :].rearrange("p k b -> p (k b)"), x1keep[:, :], q1[:, :],
                                      ALU.add).then_inc(x2_ready, 1)
                if s == 2:
                    reset(gru)
                if s == 3:
                    weigh(gru)
                split_tanh((s + 1) % 4, 0, now, tanh_ready[s][0], now)
                if s == 2:
                    argument(gru, u)
                if s == 3:
                    new_h(gru)
                split_tanh((s + 1) % 4, 1, now, tanh_ready[s][1], now)
                if u == UNROLL - 1 and s == 2:
                    bias_inputs(RZ, at(3 * UNROLL))
                if u == 0 and s == 1:
                    bias_inputs(N, at(2 * UNROLL))
                if u == 0 and s == 2:
                    split_x_low(at(UNROLL + 3), at(3 * UNROLL))

            ahead = counts(dve, 0)
            window(ahead, 0, 0, first=True)
            turns = [(u, s) for u in range(UNROLL) for s in range(4)]
            with dve.Fori(0, T - 2 * UNROLL + 1, UNROLL) as t:
                at = counts(dve, t)
                for u, s in turns[1:] + [(UNROLL, 0)]:
                    window(at, u, s)
            ahead = counts(dve, T - UNROLL)
            for u, s in turns[1:]:
                window(ahead, u, s)
            dve.wait_ge(q1raw_ready, T)
            dve.tensor_scalar(q1[:, :], q1raw[:, :], CLAMP, -CLAMP, ALU.min, ALU.max).then_inc(q1_ready, 1)
            dve.wait_ge(q1_ready, T + 1)
            dve.wait_ge(x1keep_ready, T)
            dve.tensor_tensor(xT[:, T - 1, :, :].rearrange("p k b -> p (k b)"), x1keep[:, :], q1[:, :],
                              ALU.add).then_inc(x2_ready, 1)

            dve.wait_ge(x2_ready, T + 1)
            for n in range(BLOCKS):
                dve.tensor_reduce(blk[:, :, :, n], xT[:, n * BLOCK:(n + 1) * BLOCK, :, :].rearrange("p t k b -> p k b t"),
                                  AX.X, ALU.add).then_inc(blk_ready, 1)
            then = link

            def rsqrt(rows_n, cols, var_done, root_sem, v, out_ap):
                dve.wait_ge(root_sem, v)
                a, r, w = newton[0:rows_n, 0, 0:cols], newton[0:rows_n, 1, 0:cols], newton[0:rows_n, 2, 0:cols]
                then(dve.reciprocal(r, root[0:rows_n, 0:cols]))
                then(dve.tensor_tensor(w, r, r, ALU.mult))
                then(dve.tensor_tensor(w, w, a, ALU.mult))
                then(dve.tensor_scalar(w, w, -0.5, 1.5, ALU.mult, ALU.add))
                then(dve.tensor_tensor(out_ap, r, w, ALU.mult))

            then(dve.tensor_tensor(keyq[0:NB, :], rms_row[0:NB, :], query_row[0:NB, :], ALU.mult))
            dve.wait_ge(sumsq_ready, 1)
            then(dve.tensor_tensor(scratch[0:NB, :], pwork[0][0:NB, :], keyq[0:NB, :], ALU.mult))
            then(dve.tensor_reduce(dot[:, :], scratch[0:NB, :], AX.X, ALU.add))
            dve.tensor_scalar(newton[0:NB, 0, 0:1], sumsq[:, :], 1.0 / D, L2_EPS, ALU.mult, ALU.add).then_inc(var_ready, 1)
            rsqrt(NB, 1, None, root_ready, 1, newton[0:NB, 1, 1:2])
            dve.tensor_tensor(score[:, :], dot[:, :], newton[0:NB, 1, 1:2], ALU.mult).then_inc(score_ready, 1)
            dve.wait_ge(srow_mm, 1)
            then(dve.tensor_copy(srow[:, 0, :, :].rearrange("p b n -> p (b n)"), pscore[0:1, 0:NB]))
            then(dve.tensor_reduce(smax[:, 0, :], srow[:, 0, :, :], AX.X, ALU.max))
            dve.tensor_tensor(srow[:, 1, :, :], srow[:, 0, :, :], smax[:, 0, :].unsqueeze(2).broadcast_to([1, B, BLOCKS]),
                              ALU.subtract).then_inc(sexp_in, 1)
            dve.wait_ge(sexp_ready, 1)
            then(dve.tensor_reduce(smax[:, 1, :], srow[:, 2, :, :], AX.X, ALU.add))
            then(dve.reciprocal(smax[:, 2, :], smax[:, 1, :]))
            dve.tensor_tensor(srow[:, 3, :, :], srow[:, 2, :, :], smax[:, 2, :].unsqueeze(2).broadcast_to([1, B, BLOCKS]),
                              ALU.mult).then_inc(attn_ready, 1)
            dve.wait_ge(attn_mm, 1)
            then(dve.tensor_tensor(weighted[:, :, :, :].rearrange("p k b n -> p k (b n)"),
                                   blk[:, :, :, :].rearrange("p k b n -> p k (b n)"),
                                   pwork[1][:, 0:NB].unsqueeze(1).broadcast_to([P, K, NB]), ALU.mult))
            dve.tensor_reduce(att[:, :, :], weighted[:, :, :, :], AX.X, ALU.add).then_inc(att_ready, 1)

            def turn_to_weights(b):
                for k in range(K):
                    e = b * K + k
                    dve.wait_ge(dist_ready, e + 1)
                    dve.tensor_scalar(spread[:, b, k, :], spread[:, b, k, :], 1.0, 1.0, ALU.min, ALU.subtract).then_inc(spread_ready, 1)

            def moments_of(b, tiles):
                dve.wait_ge(projb_ready, b + 1)
                for n in tiles:
                    e = b * K + n
                    dve.wait_ge(x2s_ready, e + 1)
                    if b >= 1:
                        dve.wait_ge(normed_ready, e - K + 1)
                    dve.tensor_tensor(ytile[:, n, :], x2s[b % 2][:, n, :], projb[:, b, :], ALU.add).then_inc(y_ready, 1)
                for n in tiles:
                    dve.wait_ge(y_ready, b * K + n + 1)
                    dve.bn_stats(stats[:, n, :], ytile[:, n, :]).then_inc(stats_ready, 1)
                for n in tiles:
                    dve.wait_ge(stats_ready, b * K + n + 1)
                    ins = dve.bn_aggr(moments[:, b % 2, n, :], stats[:, n, :])
                link(ins)

            def scale_of(b):
                dve.tensor_scalar(newton[:, 0, :], moments[:, b % 2, :, 1], L2_EPS, None, ALU.add).then_inc(var_ready, 1)
                rsqrt(P, K, None, root_ready, b + 2, rstd[:, b % 2, :])
                dve.scalar_tensor_tensor(shift[:, b % 2, :], moments[:, b % 2, :, 0], -1.0, rstd[:, b % 2, :],
                                         ALU.mult, ALU.mult).then_inc(rstd_ready, 1)
                dve.wait_ge(rstd_ready, b + 1)

            def add_x2(b, n):
                e = b * K + n
                dve.wait_ge(normed_ready, e + 1)
                dve.tensor_tensor(x3[:, b % 2, n, :], normed[:, b % 2, n, :], gamma_row, ALU.mult).then_inc(scaled_ready, 1)
                dve.wait_ge(shifted_ready, e + 1)
                dve.wait_ge(scaled_ready, e + 1)
                dve.tensor_tensor(x3[:, b % 2, n, :], x3[:, b % 2, n, :], x2s[b % 2][:, n, :], ALU.add).then_inc(x3_ready, 1)

            turn_to_weights(0)
            dve.wait_ge(mats_ready, 2 * K)
            dve.wait_ge(proj_mm, 1)
            moments_of(0, range(K))
            scale_of(0)
            for n in range(K):
                add_x2(0, n)
            moments_of(1, range(K))
            scale_of(1)
            turn_to_weights(1)
            for b in range(B):
                for n in range(K):
                    e = b * K + n
                    if b + 1 < B:
                        add_x2(b + 1, n)
                    if b + 2 < B:
                        moments_of(b + 2, [n])
                    dve.wait_ge(x3_ready, e + 1)
                    dve.wait_ge(sample_mm, e + 1)
                    dve.tensor_tensor(normed[:, b % 2, n, :], x3[:, b % 2, n, :], pwork[e % 2][:, :],
                                      ALU.subtract).then_inc(final_ready, 1)
                if b + 2 < B:
                    scale_of(b + 2)
                    turn_to_weights(b + 2)

        @block.tensor
        def _(pe):
            pe.wait_ge(ident_ready, 1)

            def turn_x(b):
                pe.wait_ge(in_x[b % 2], 16 * (b // 2 + 1))
                for n in range(K):
                    e = b * K + n
                    if e >= 4:
                        pe.wait_ge(xT_ready, e - 3)
                    for k in range(K):
                        mm = pe.transpose(bounce[e % 4][:, k * P:(k + 1) * P], xrow[:, b % 2, n, k * P:(k + 1) * P],
                                          ident[:, :])
                    mm.then_inc(turned, 1)

            pe.wait_ge(in_small, 64)
            pe.transpose(pwork[0][:, 0:NS], small, ident[0:NS, 0:NS]).then_inc(small_turned, 1)
            pe.wait_ge(consts_ready, 1)
            pe.wait_ge(in_c, 16)
            for k in range(K):
                for n in range(K):
                    mm = pe.transpose(cbank[k][:, n * P:(n + 1) * P], c_row[:, n, k * P:(k + 1) * P], ident[:, :])
                mm.then_inc(cturned, 1)
            for b in range(B):
                turn_x(b)

            def input_products(tiles):
                for n in tiles:
                    for k in range(K):
                        for w in range(2):
                            mm = pe.matmul(pgi[:, n * 2 * XC:(n + 1) * 2 * XC], wihp[:, w, k, n * P:(n + 1) * P],
                                           xpart[:, :, :].rearrange("p a (t c) -> p (a t) c", c=KB)[:, :, k * B:(k + 1) * B],
                                           start=(n == 0 and k == 0 and w == 0),
                                           stop=(n == G3 - 1 and k == K - 1 and w == 1), skip_group_check=True)
                    if n == 2 * K - 1:
                        mm.then_inc(gi_mm[0], UNROLL)
                    if n == G3 - 1:
                        mm.then_inc(gi_mm[1], UNROLL)

            def gates_mm(c):
                n = GATE_ORDER[c]
                part, col, last = (0, c * B, 2 * K - 1) if c < 2 * K else (1, (c - 2 * K) * B, G3 - 1)
                for k in range(K):
                    for w in range(2):
                        mm = pe.matmul(gate_out[part][:, :, col:col + B], whh[:, w, k, n * P:(n + 1) * P],
                                       hpart[:, k, :, :], start=(col == 0 and k == 0 and w == 0),
                                       stop=(c == last and k == K - 1 and w == 1), skip_group_check=True)
                if c == 2 * K - 1:
                    mm.then_inc(nr_mm, 1)
                if c == G3 - 1:
                    mm.then_inc(z_mm, 1)

            pe.wait_ge(whh_ready, 1)
            pe.wait_ge(wih_ready, 1)
            pe.wait_ge(cpl_ready, 1)
            pe.wait_ge(x_parts, UNROLL)
            input_products(range(G3))
            for v in (1, 2):
                pe.wait_ge(h_parts, v)
                for c in range(G3):
                    gates_mm(c)
            pe.wait_ge(x_parts, 2 * UNROLL)
            pe.wait_ge(z_sum, 2)
            input_products(range(G3))

            def stage_products(s, ks, ns):
                for n in ns:
                    a, col = n // HK, n % HK * B
                    for k in ks:
                        for w in range(2):
                            mm = pe.matmul(stage_out[a][:, :, col:col + B], cpl[:, w, k, n * P:(n + 1) * P],
                                           tpart[:, s % 2, k, :, :], start=(col == 0 and k == 0 and w == 0),
                                           stop=(n % HK == HK - 1 and k == K - 1 and w == 1), skip_group_check=True)
                return mm

            k_first, k_second = range(HK), range(HK, K)

            def step(at, u):
                now, tail, gru = at(u + 1), at(u + 2), at(u + 3)
                for s in range(4):
                    pe.wait_ge(t_parts[s][0], now)
                    stage_products(s, k_first, range(HK + 1))
                    pe.wait_ge(t_parts[s][1], now)
                    stage_products(s, k_second, range(HK)).then_inc(stage_mm[s][0], 1)
                    stage_products(s, k_first, range(HK + 1, K))
                    stage_products(s, k_second, range(HK, K)).then_inc(stage_mm[s][1], 1)
                    if s == 0:
                        pe.wait_ge(h_parts, gru)
                    for c in GATES_AFTER[s]:
                        gates_mm(c)
                    if s == 3:
                        if u == 0:
                            pe.wait_ge(x_parts, at(3 * UNROLL))
                        pe.wait_ge(z_sum, gru)
                        input_products(range(u * G3 // UNROLL, (u + 1) * G3 // UNROLL))

            with pe.Fori(0, T - UNROLL + 1, UNROLL) as t:
                at = counts(pe, t)
                for u in range(UNROLL):
                    step(at, u)

            pe.wait_ge(in_mats, 32)
            for k in range(2 * K):
                if k == 0:
                    pe.wait_ge(stage_sum[3][1], T)
                if k >= 4:
                    pe.wait_ge(mats_ready, k - 3)
                for n in range(K):
                    row = wk_row if k < K else wo_row
                    mm = pe.transpose(bounce[k % 4][:, n * P:(n + 1) * P], row[:, n, (k % K) * P:(k % K + 1) * P], ident[:, :])
                mm.then_inc(mats_turned, 1)

            def turn_x2(b, n):
                e = b * K + n
                if e < 2:
                    pe.wait_ge(mats_ready, K + 1 + e)
                else:
                    pe.wait_ge(x2s_ready, e - 1)
                if 2 * K <= e < 2 * K + 2:
                    pe.wait_ge(projb_ready, B)
                for k in range(K):
                    mm = pe.transpose(bounce[e % 2][:, k * P:(k + 1) * P], xT[:, n * P:(n + 1) * P, k, b], ident[:, :])
                mm.then_inc(x2_turned, 1)

            pe.wait_ge(x2_ready, T + 1)
            for b in range(2):
                for n in range(K):
                    turn_x2(b, n)
            pe.wait_ge(blk_ready, BLOCKS)
            pe.wait_ge(mats_ready, 2 * K)
            for k in range(K):
                mm = pe.matmul(pwork[0][0:NB, :], blk[:, k, :, :].rearrange("p b n -> p (b n)"), wkT[:, k, :],
                               start=(k == 0), stop=(k == K - 1))
            mm.then_inc(keys_mm, 1)
            pe.wait_ge(score_ready, 1)
            pe.matmul(pscore[0:1, 0:NB], score[:, :], ident[0:NB, 0:NB], start=True, stop=True).then_inc(srow_mm, 1)
            pe.wait_ge(pick_ready, 2)
            pe.wait_ge(attn_ready, 1)
            pe.matmul(pwork[1][:, 0:NB], onerow[:, :], srow[:, 3, :, :].rearrange("p b n -> p (b n)"),
                      start=True, stop=True).then_inc(attn_mm, 1)
            pe.wait_ge(att_ready, 1)
            for k in range(K):
                mm = pe.matmul(pwork[2][0:B, :], att[:, k, :], woT[:, k, :], start=(k == 0), stop=(k == K - 1))
            mm.then_inc(proj_mm, 1)
            pe.wait_ge(x2s_ready, 2 * K)
            pe.wait_ge(proj4_ready, 1)
            for b in range(B):
                pe.matmul(bounce[b], pick[:, b, :], proj4, start=True, stop=True).then_inc(projb_mm, 1)

            def turn_x3(e):
                b, n = divmod(e, K)
                pe.wait_ge(x3_ready, e + 1)
                if e >= 2:
                    pe.wait_ge(x3T_ready, e - 1)
                for k in range(K):
                    mm = pe.transpose(bounce[2 + e % 2][:, k * P:(k + 1) * P], x3[:, b % 2, n, k * P:(k + 1) * P], ident[:, :])
                mm.then_inc(x3_turned, 1)

            turn_x3(0)
            for e in range(B * K):
                b, n = divmod(e, K)
                if n < K - 1:
                    turn_x3(e + 1)
                if b + 2 < B:
                    turn_x2(b + 2, n)
                pe.wait_ge(x3T_ready, e + 1)
                if e >= 2:
                    pe.wait_ge(final_ready, e - 1)
                pe.wait_ge(spread_ready, K * (b + 1))
                for k in range(K):
                    mm = pe.matmul(pwork[e % 2][:, :], x3T[:, e % 2, k, :], spread[:, b, k, :],
                                   start=(k == 0), stop=(k == K - 1))
                mm.then_inc(sample_mm, 1)
                if n == K - 1 and b + 1 < B:
                    turn_x3(e + 1)


_INS = ['x', 'cond_2048', 'L0_cond_W_ih', 'L0_cond_W_hh', 'L0_cond_b_ih', 'L0_cond_b_hh', 'L1_cond_coupling',
        'L1_cond_bias', 'L2_cond_rms_weight', 'L2_cond_Wk', 'L2_cond_Wo', 'L2_cond_ln_gamma', 'L2_cond_ln_beta']
_OUTS = [((B, T, D), 'float32')]


def kernel(**inputs):
    import numpy as _np
    import concourse.bacc as _bacc
    from concourse import mybir as _mybir
    from concourse.bass_utils import run_bass_kernel_spmd as _run

    nc = _bacc.Bacc("TRN2", target_bir_lowering=False, num_devices=1)
    arrays, args = {}, []
    for name in _INS:
        a = _np.ascontiguousarray(inputs[name])
        arrays[f"in_{name}_dram"] = a
        args.append(nc.dram_tensor(f"in_{name}_dram", a.shape, _mybir.dt.from_np(a.dtype), kind="ExternalInput").ap())
    for i, (shape, dtype) in enumerate(_OUTS):
        dt = _mybir.dt.from_np(_np.dtype(dtype))
        args.append(nc.dram_tensor(f"out_{i}_dram", shape, dt, kind="ExternalOutput").ap())
    build(nc, *args)
    r = _run(nc, [arrays], core_ids=[0])
    got = tuple(r.results[0][f"out_{i}_dram"] for i in range(len(_OUTS)))
    return got[0]
```
